# Optimizing a Trainium2 kernel written in Bass

```python
import numpy as np
import jax
import jax.numpy as jnp

def _softmax(x, axis=-1):
    return jax.nn.softmax(x, axis=axis)

def _gelu(x):
    return jax.nn.gelu(x, approximate=True)

def _silu(x):
    return jax.nn.silu(x)

def _sigmoid(x):
    return jax.nn.sigmoid(x)

def _layernorm(x, axis=-1, eps=1e-05):
    m = jnp.mean(x, axis=axis, keepdims=True)
    v = jnp.var(x, axis=axis, keepdims=True)
    return (x - m) / jnp.sqrt(v + eps)

def _scatter_add(tgt, idx, src, axis=0):
    return tgt.at[idx].add(src)

def _segment_sum(src, seg, n):
    return jax.ops.segment_sum(src, seg, n)
kernel_name = 'mk_conv_seq_d2_conv_nchw256_r2_4aa511'

def setup_inputs(seed: int=0):
    np.random.seed(seed)
    _w = jnp.asarray

    def _rec_inputs():
        import jax
        import jax.numpy as jnp
        _gk = jax.random.key(seed)
        x = -0.0002928 + 1 * jax.random.normal(jax.random.fold_in(_gk, 1), (4, 128, 32, 32), jnp.float32)
        return x
    x = _rec_inputs()

    def _L0_conv_setup():
        import jax, jax.numpy as jnp
        import numpy as np
        IN_C = 128
        INTER_C = 64

        def _conv1x1(x_flat, w, b):
            return jnp.einsum('oc,bcn->bon', w, x_flat) + b[None, :, None]
        key = jax.random.key(seed)
        ks = jax.random.split(key, 9)
        x = jax.random.normal(ks[0], (4, IN_C, 32, 32), dtype=jnp.float32)
        s_in = 1.0 / np.sqrt(IN_C)
        s_mid = 1.0 / np.sqrt(INTER_C)
        return {'x': x, 'g_w': jax.random.uniform(ks[1], (INTER_C, IN_C), jnp.float32, -s_in, s_in), 'g_b': jax.random.uniform(ks[2], (INTER_C,), jnp.float32, -s_in, s_in), 'theta_w': jax.random.uniform(ks[3], (INTER_C, IN_C), jnp.float32, -s_in, s_in), 'theta_b': jax.random.uniform(ks[4], (INTER_C,), jnp.float32, -s_in, s_in), 'phi_w': jax.random.uniform(ks[5], (INTER_C, IN_C), jnp.float32, -s_in, s_in), 'phi_b': jax.random.uniform(ks[6], (INTER_C,), jnp.float32, -s_in, s_in), 'out_w': jax.random.uniform(ks[7], (IN_C, INTER_C), jnp.float32, -s_mid, s_mid), 'out_b': jax.random.uniform(ks[8], (IN_C,), jnp.float32, -s_mid, s_mid)}
    _L0_conv_all = _L0_conv_setup()
    _L0_conv_in = {k: v for k, v in _L0_conv_all.items() if k in ('g_w', 'g_b', 'theta_w', 'theta_b', 'phi_w', 'phi_b', 'out_w', 'out_b')}
    del _L0_conv_all

    def _L1_conv_setup():
        import jax, jax.numpy as jnp
        import numpy as np
        N, C, H, W = (4, 128, 32, 32)

        def conv1x1(x, w, b):
            return jnp.einsum('nchw,oc->nohw', x, w) + b[None, :, None, None]
        key = jax.random.key(seed)
        ks = jax.random.split(key, 4)
        scale = 1.0 / np.sqrt(C)
        return {'x': jax.random.normal(ks[0], (N, C, H, W), dtype=jnp.float32), 'theta_w': jax.random.normal(ks[1], (C, C), dtype=jnp.float32) * scale, 'theta_b': jnp.zeros((C,), dtype=jnp.float32), 'phi_w': jax.random.normal(ks[2], (C, C), dtype=jnp.float32) * scale, 'phi_b': jnp.zeros((C,), dtype=jnp.float32), 'conv1_w': jax.random.normal(ks[3], (C, C), dtype=jnp.float32) * scale, 'conv1_b': jnp.zeros((C,), dtype=jnp.float32)}
    _L1_conv_all = _L1_conv_setup()
    _L1_conv_in = {k: v for k, v in _L1_conv_all.items() if k in ('theta_w', 'theta_b', 'phi_w', 'phi_b', 'conv1_w', 'conv1_b')}
    del _L1_conv_all
    return {'x': x, 'L0_conv_g_w': _L0_conv_in['g_w'], 'L0_conv_g_b': _L0_conv_in['g_b'], 'L0_conv_theta_w': _L0_conv_in['theta_w'], 'L0_conv_theta_b': _L0_conv_in['theta_b'], 'L0_conv_phi_w': _L0_conv_in['phi_w'], 'L0_conv_phi_b': _L0_conv_in['phi_b'], 'L0_conv_out_w': _L0_conv_in['out_w'], 'L0_conv_out_b': _L0_conv_in['out_b'], 'L1_conv_theta_w': _L1_conv_in['theta_w'], 'L1_conv_theta_b': _L1_conv_in['theta_b'], 'L1_conv_phi_w': _L1_conv_in['phi_w'], 'L1_conv_phi_b': _L1_conv_in['phi_b'], 'L1_conv_conv1_w': _L1_conv_in['conv1_w'], 'L1_conv_conv1_b': _L1_conv_in['conv1_b']}

def reference(x, L0_conv_g_w, L0_conv_g_b, L0_conv_theta_w, L0_conv_theta_b, L0_conv_phi_w, L0_conv_phi_b, L0_conv_out_w, L0_conv_out_b, L1_conv_theta_w, L1_conv_theta_b, L1_conv_phi_w, L1_conv_phi_b, L1_conv_conv1_w, L1_conv_conv1_b):
    import jax
    import jax.numpy as jnp

    def _L0_conv_ref(x, g_w, g_b, theta_w, theta_b, phi_w, phi_b, out_w, out_b):
        import jax, jax.numpy as jnp
        import numpy as np
        IN_C = 128
        INTER_C = 64

        def _conv1x1(x_flat, w, b):
            return jnp.einsum('oc,bcn->bon', w, x_flat) + b[None, :, None]
        n, c, h, w = x.shape
        N = h * w
        x_flat = x.reshape(n, c, N)
        g_x = _conv1x1(x_flat, g_w, g_b).transpose(0, 2, 1)
        theta_x = _conv1x1(x_flat, theta_w, theta_b).transpose(0, 2, 1)
        phi_x = _conv1x1(x_flat, phi_w, phi_b)
        pairwise_weight = jnp.matmul(theta_x, phi_x) / N
        y = jnp.matmul(pairwise_weight, g_x)
        y = y.transpose(0, 2, 1)
        out = x_flat + _conv1x1(y, out_w, out_b)
        return out.reshape(n, c, h, w)

    def _L1_conv_ref(x, theta_w, theta_b, phi_w, phi_b, conv1_w, conv1_b):
        import jax, jax.numpy as jnp
        import numpy as np
        N, C, H, W = (4, 128, 32, 32)

        def conv1x1(x, w, b):
            return jnp.einsum('nchw,oc->nohw', x, w) + b[None, :, None, None]
        n, c, h, w = x.shape
        hw = h * w
        theta = conv1x1(x, theta_w, theta_b).reshape(n, c, hw)
        phi = conv1x1(x, phi_w, phi_b).reshape(n, c, hw)
        g = x.reshape(n, c, hw)
        scores = jnp.einsum('ncp,ncq->npq', theta, phi) / jnp.sqrt(jnp.asarray(c, x.dtype))
        attn = jax.nn.softmax(scores, axis=-1)
        f = jnp.einsum('npq,ncq->ncp', attn, g).reshape(n, c, h, w)
        result = conv1x1(f, conv1_w, conv1_b)
        return x + result

    def _gn(v, G=32, eps=1e-05):
        B_, C_, H_, W_ = v.shape
        g = v.reshape(B_, G, C_ // G, H_, W_)
        m = jnp.mean(g, axis=(2, 3, 4), keepdims=True)
        s = jnp.var(g, axis=(2, 3, 4), keepdims=True)
        return ((g - m) / jnp.sqrt(s + eps)).reshape(v.shape)

    def _ln_c(v, eps=1e-06):
        m = jnp.mean(v, axis=1, keepdims=True)
        s = jnp.var(v, axis=1, keepdims=True)
        return (v - m) / jnp.sqrt(s + eps)

    def _ln_t(v, eps=1e-05):
        m = jnp.mean(v, axis=-1, keepdims=True)
        s = jnp.var(v, axis=-1, keepdims=True)
        return (v - m) / jnp.sqrt(s + eps)

    def _to_tokens(v):
        B_, C_, H_, W_ = v.shape
        return v.reshape(B_, C_, H_ * W_).transpose(0, 2, 1)

    def _from_tokens(t, like):
        B_, C_, H_, W_ = like.shape
        return t.transpose(0, 2, 1).reshape(B_, C_, H_, W_)
    x = _L0_conv_ref(x, L0_conv_g_w, L0_conv_g_b, L0_conv_theta_w, L0_conv_theta_b, L0_conv_phi_w, L0_conv_phi_b, L0_conv_out_w, L0_conv_out_b)
    x = _L1_conv_ref(x, L1_conv_theta_w, L1_conv_theta_b, L1_conv_phi_w, L1_conv_phi_b, L1_conv_conv1_w, L1_conv_conv1_b)
    return x

_drawn_inputs = setup_inputs


def setup_inputs(seed=0):
    import zlib

    import numpy as np

    out = dict(_drawn_inputs(seed))
    spreads = {'L1_conv_theta_b': (0.0, 0.795),
     'L1_conv_phi_b': (0.0, 0.8),
     'L1_conv_conv1_b': (0.0, 0.1)}
    factors = {'L0_conv_g_b': 6.292, 'L0_conv_theta_b': 5.277, 'L0_conv_phi_b': 6.977}
    for name, (base, spread) in spreads.items():
        noise = np.random.default_rng([zlib.crc32(name.encode()), seed]).standard_normal(out[name].shape)
        drawn = base * np.exp(spread * noise) if base else spread * noise
        out[name] = jnp.asarray(drawn.astype(out[name].dtype))
    for name, factor in factors.items():
        out[name] = (out[name] * factor).astype(out[name].dtype)
    return out
```

```python
from contextlib import ExitStack

import concourse.bass as bass
from concourse import mybir

F32 = mybir.dt.float32
F32R = mybir.dt.float32r
ALU = mybir.AluOpType
ACT = mybir.ActivationFunctionType
AX = mybir.AxisListType

IMAGES = 4
C = 128
CI = 64
PIX = 1024
TILE = 128
TILES = PIX // TILE
BANK = 512
GROUPS = PIX // BANK
GT = TILES // GROUPS
PIECES = 4
CHUNKS_PER_PIECE = TILES // PIECES

W_PG, W_T, W_P, W_C = 0, C, 2 * C, 3 * C
B_T, B_P, B_C, B_O = 4 * C, 4 * C + 1, 4 * C + 2, 4 * C + 3
W_COLS = 4 * C + 4
I_T, I_O, I_TB = 0, C, 2 * C
I_COLS = 2 * C + 1


def build(nc, x, weights, inner, pg_bias, out):
    with ExitStack() as ctx:
        def sb(name, shape, dt=F32):
            return ctx.enter_context(nc.sbuf_tensor(name, shape, dt))

        def sem(name):
            return ctx.enter_context(nc.semaphore(name))

        w = sb("w", [C, W_COLS])
        wi = sb("wi", [CI, I_COLS])
        pg_b = sb("pg_b", [C, C])
        phi_w = sb("phi_w", [C, C])
        phi_b = sb("phi_b", [C, 1])
        identity = sb("identity", [C, C])
        X = sb("X", [C, PIX])
        pgT = sb("pgT", [C, TILES, C])
        MT = sb("MT", [CI, C])
        R = sb("R", [CI, C])
        AT = sb("AT", [C, C])
        d = sb("d", [C, 1])
        Z = sb("Z", [C, PIX])
        Zres = sb("Zres", [C, PIX])
        T_hi, T_lo = sb("T_hi", [C, PIX], F32R), sb("T_lo", [C, PIX], F32R)
        Phi_hi, Phi_lo = sb("Phi_hi", [C, PIX], F32R), sb("Phi_lo", [C, PIX], F32R)
        V_hi, V_lo = sb("V_hi", [C, TILES, C], F32R), sb("V_lo", [C, TILES, C], F32R)
        negmax = sb("negmax", [C, TILES])
        den = sb("den", [C, TILES])
        rden = sb("rden", [C, TILES])
        P = sb("P", [C, 2, PIX])
        PT_hi = sb("PT_hi", [C, GROUPS, TILES, BANK], F32R)
        PT_lo = sb("PT_lo", [C, GROUPS, TILES, BANK], F32R)
        rdenB = sb("rdenB", [C, BANK])
        scaled = sb("scaled", [C, GROUPS, BANK])
        result = sb("result", [C, GROUPS, BANK])

        ring = ctx.enter_context(nc.psum_tensor("ring", [C, 2, PIX], F32))
        turned = ctx.enter_context(nc.psum_tensor("turned", [C, PIX], F32))
        numer = ctx.enter_context(nc.psum_tensor("numer", [C, BANK], F32))
        small = ctx.enter_context(nc.psum_tensor("small", [C, BANK], F32))

        S_SLOT = [0, 1, 1, 1, 0, 0, 0, 1]
        PG_SLOT, M_SLOT, V_SLOT, AX_SLOT, T_SLOT, PHI_SLOT = 0, 0, 1, 1, 0, 1

        w_loaded = sem("w_loaded")
        x_loaded = sem("x_loaded")
        identity_ready, pad_ready = sem("identity_ready"), sem("pad_ready")
        phi_w_ready = sem("phi_w_ready")
        pg_ready, pg_copied = sem("pg_ready"), sem("pg_copied")
        m_ready, m_copied = sem("m_ready"), sem("m_copied")
        r_ready, r_copied = sem("r_ready"), sem("r_copied")
        a_ready, a_copied = sem("a_ready"), sem("a_copied")
        ax_ready, z_ready, zres_ready = sem("ax_ready"), sem("z_ready"), sem("zres_ready")
        t_ready, t_hi, t_lo = sem("t_ready"), sem("t_hi"), sem("t_lo")
        phi_ready, phi_hi, phi_lo = sem("phi_ready"), sem("phi_hi"), sem("phi_lo")
        v_ready, v_hi, v_lo = sem("v_ready"), sem("v_hi"), sem("v_lo")
        scores_ready, max_ready, probs_ready = sem("scores_ready"), sem("max_ready"), sem("probs_ready")
        turned_ready, turned_hi, turned_lo = sem("turned_ready"), sem("turned_hi"), sem("turned_lo")
        pieces_done = sem("pieces_done")
        rden_ready, rden_spread, rden_copied = sem("rden_ready"), sem("rden_spread"), sem("rden_copied")
        scaled_ready, result_ready = sem("scaled_ready"), sem("result_ready")
        stored = [sem(f"stored{g}") for g in range(GROUPS)]

        block = ctx.enter_context(nc.Block())

        def over_images(eng, image):
            image(0, False, True)
            with eng.Fori(1, IMAGES - 1) as b:
                image(b, True, True)
            image(IMAGES - 1, True, False)

        @block.sync
        def _(sp):
            sp.dma_start(X[:, :], x[0]).then_inc(x_loaded, 16)
            sp.dma_start(wi[:, :], inner).then_inc(w_loaded, 16)

            def load(b):
                sp.wait_ge(z_ready, b)
                sp.dma_start(X[:, :], x[b]).then_inc(x_loaded, 16)

            def store(b):
                for g in range(GROUPS):
                    sp.wait_ge(result_ready, b * GROUPS + g + 1)
                    sp.dma_start(out[b, :, g * BANK:(g + 1) * BANK], result[:, g, :]).then_inc(stored[g], 16)

            load(1)
            with sp.Fori(0, IMAGES - 2) as b:
                load(b + 2)
                store(b)
            store(IMAGES - 2)
            store(IMAGES - 1)
            for g in range(GROUPS):
                sp.wait_ge(stored[g], 16 * IMAGES)

        @block.tensor
        def _(pe):
            def phi_g(b):
                pe.wait_ge(x_loaded, (b + 1) * 16)
                for j in range(TILES):
                    mm = nc.tensor.matmul(ring[:, PG_SLOT, j * C:(j + 1) * C], X[:, j * TILE:(j + 1) * TILE],
                                          w[:, W_PG:W_PG + C], start=True, stop=True)
                mm.then_inc(pg_ready, 1)

            def inner_product(b):
                pe.wait_ge(pg_copied, b + 1)
                for j in range(TILES):
                    mm = nc.tensor.matmul(ring[0:CI, M_SLOT, 0:CI], pgT[:, j, CI:C], pgT[:, j, 0:CI],
                                          start=(j == 0), stop=(j == TILES - 1))
                mm.then_inc(m_ready, 1)

            def out_times_inner(b):
                pe.wait_ge(m_copied, b + 1)
                nc.tensor.matmul(small[:, 0:C], MT[:, :], wi[:, I_O:I_O + C],
                                 start=True, stop=True).then_inc(r_ready, 1)

            def fold(b):
                pe.wait_ge(r_copied, b + 1)
                nc.tensor.matmul(small[:, 0:C], wi[:, I_T:I_T + C], R[:, :], start=True, stop=True)
                nc.tensor.matmul(small[:, C:C + 1], R[:, :], wi[:, I_TB:I_TB + 1],
                                 start=True, stop=True).then_inc(a_ready, 1)

            def conv(slot, weight, source, done):
                for h in range(GROUPS):
                    mm = nc.tensor.matmul(ring[:, slot, h * BANK:(h + 1) * BANK], weight,
                                          source[:, h * BANK:(h + 1) * BANK], start=True, stop=True)
                mm.then_inc(done, 1)

            def values(b):
                pe.wait_ge(probs_ready, b * TILES + 4)
                for j in range(TILES):
                    mm = nc.tensor.matmul(ring[:, V_SLOT, j * C:(j + 1) * C], Z[:, j * TILE:(j + 1) * TILE],
                                          w[:, W_C:W_C + C], start=True, stop=True)
                mm.then_inc(v_ready, 1)

            def scores(t):
                slot = S_SLOT[t]
                rows = slice(t * TILE, (t + 1) * TILE)
                for n, (left, right) in enumerate(((T_hi, Phi_hi), (T_hi, Phi_lo), (T_lo, Phi_hi))):
                    for h in range(GROUPS):
                        cols = slice(h * BANK, (h + 1) * BANK)
                        mm = nc.tensor.matmul(ring[:, slot, cols], left[:, rows], right[:, cols],
                                              start=(n == 0), stop=(n == 2))
                mm.then_inc(scores_ready, 1)

            def turn(b, t, first=False):
                pe.wait_ge(probs_ready, b * TILES + t + 1)
                if not first:
                    pe.wait_ge(turned_lo, b * TILES + t)
                for j in range(TILES):
                    mm = nc.tensor.transpose(turned[:, j * TILE:(j + 1) * TILE],
                                             P[:, t % 2, j * TILE:(j + 1) * TILE], identity[:, :])
                mm.then_inc(turned_ready, 1)

            def attend(b, g, i, first=False):
                if i == 0:
                    pe.wait_ge(turned_lo, b * TILES + (g + 1) * GT)
                    if g == 0:
                        pe.wait_ge(v_lo, b + 1)
                    if not first:
                        pe.wait_ge(scaled_ready, b * GROUPS + g)
                for j in range(i * CHUNKS_PER_PIECE, (i + 1) * CHUNKS_PER_PIECE):
                    for n, (left, right) in enumerate(((V_hi, PT_hi), (V_hi, PT_lo), (V_lo, PT_hi))):
                        mm = nc.tensor.matmul(numer[:, :], left[:, j, :], right[:, g, j, :],
                                              start=(j == 0 and n == 0), stop=(j == TILES - 1 and n == 2))
                mm.then_inc(pieces_done, 1)

            def spread(b, g):
                pe.wait_ge(rden_ready, b * GROUPS + g + 1)
                for k in range(GT):
                    t = g * GT + k
                    mm = nc.tensor.transpose(small[:, k * TILE:(k + 1) * TILE],
                                             rden[:, t:t + 1].broadcast_to([C, TILE]), identity[:, :])
                mm.then_inc(rden_spread, 1)

            pe.wait_ge(w_loaded, 16 * 3)
            phi_g(0)
            inner_product(0)
            pe.wait_ge(pad_ready, 1)
            out_times_inner(0)
            fold(0)
            pe.wait_ge(a_copied, 1)
            conv(AX_SLOT, AT[:, :], X, ax_ready)
            pe.wait_ge(z_ready, 1)
            conv(T_SLOT, w[:, W_T:W_T + C], Z, t_ready)
            pe.wait_ge(phi_w_ready, 2)
            conv(PHI_SLOT, phi_w[:, :], Z, phi_ready)
            pe.wait_ge(identity_ready, 2)

            def image(b, has_prev, has_next):
                if has_prev:
                    turn(b - 1, 7)
                    attend(b - 1, 0, 3)
                    pe.wait_ge(a_copied, b + 1)
                    spread(b - 1, 0)
                pe.wait_ge(t_lo, b + 1)
                pe.wait_ge(phi_lo, b + 1)
                scores(0)
                scores(1)
                turn(b, 0, first=not has_prev)
                if has_prev:
                    attend(b - 1, 1, 0)
                if has_next:
                    phi_g(b + 1)
                pe.wait_ge(probs_ready, b * TILES + 2)
                scores(2)
                turn(b, 1)
                if has_prev:
                    attend(b - 1, 1, 1)
                if has_next:
                    inner_product(b + 1)
                pe.wait_ge(probs_ready, b * TILES + 3)
                scores(3)
                turn(b, 2)
                if has_prev:
                    attend(b - 1, 1, 2)
                    pe.wait_ge(rden_copied, (b - 1) * GROUPS + 1)
                if has_next:
                    out_times_inner(b + 1)
                if has_next:
                    pe.wait_ge(m_copied, b + 2)
                scores(4)
                turn(b, 3)
                if has_prev:
                    attend(b - 1, 1, 3)
                    if has_next:
                        pe.wait_ge(r_copied, b + 2)
                    spread(b - 1, 1)
                values(b)
                if has_next:
                    if has_prev:
                        pe.wait_ge(rden_copied, (b - 1) * GROUPS + 2)
                    fold(b + 1)
                pe.wait_ge(probs_ready, b * TILES + 5)
                scores(5)
                turn(b, 4)
                attend(b, 0, 0, first=not has_prev)
                if has_next:
                    pe.wait_ge(a_copied, b + 2)
                    pe.wait_ge(v_lo, b + 1)
                    conv(AX_SLOT, AT[:, :], X, ax_ready)
                pe.wait_ge(probs_ready, b * TILES + 6)
                scores(6)
                turn(b, 5)
                attend(b, 0, 1)
                if has_next:
                    pe.wait_ge(z_ready, b + 2)
                else:
                    pe.wait_ge(v_lo, b + 1)
                scores(7)
                turn(b, 6)
                if has_next:
                    conv(T_SLOT, w[:, W_T:W_T + C], Z, t_ready)
                attend(b, 0, 2)
                if has_next:
                    pe.wait_ge(probs_ready, b * TILES + 8)
                    conv(PHI_SLOT, phi_w[:, :], Z, phi_ready)

            over_images(pe, image)
            last = IMAGES - 1
            turn(last, 7)
            attend(last, 0, 3)
            pe.wait_ge(rden_copied, last * GROUPS)
            spread(last, 0)
            for i in range(PIECES):
                attend(last, 1, i)
            pe.wait_ge(rden_copied, last * GROUPS + 1)
            spread(last, 1)

        @block.scalar
        def _(act):
            act.dma_start(w[:, :], weights).then_inc(w_loaded, 16)
            act.dma_start(pg_b[:, :], pg_bias.broadcast_to([C, C])).then_inc(w_loaded, 16)

            def copy_m(b):
                act.wait_ge(m_ready, b + 1)
                nc.scalar.activation(MT[:, 0:CI], ring[0:CI, M_SLOT, 0:CI], ACT.Copy,
                                     scale=1.0 / PIX).then_inc(m_copied, 1)

            def copy_r(b):
                act.wait_ge(r_ready, b + 1)
                nc.scalar.activation(R[:, :], small[0:CI, 0:C], ACT.Copy).then_inc(r_copied, 1)

            def copy_a(b):
                act.wait_ge(a_ready, b + 1)
                nc.scalar.activation(d[:, :], small[:, C:C + 1], ACT.Identity, bias=w[:, B_O:B_O + 1])
                nc.scalar.activation(AT[:, :], small[:, 0:C], ACT.Copy).then_inc(a_copied, 1)

            def high(t_or_phi, slot, ready, bias, done, b):
                act.wait_ge(ready, b + 1)
                nc.scalar.activation(t_or_phi[:, :], ring[:, slot, :], ACT.Identity, bias=bias).then_inc(done, 1)

            def high_t(b):
                high(T_hi, T_SLOT, t_ready, w[:, B_T:B_T + 1], t_hi, b)

            def high_phi(b):
                high(Phi_hi, PHI_SLOT, phi_ready, phi_b[:, :], phi_hi, b)

            def high_v(b, has_prev):
                if has_prev:
                    act.wait_ge(pieces_done, b * PIECES * GROUPS)
                act.wait_ge(v_ready, b + 1)
                nc.scalar.activation(V_hi[:, :, :].rearrange("p j c -> p (j c)"), ring[:, V_SLOT, :],
                                     ACT.Copy).then_inc(v_hi, 1)

            def exps(b, t, has_prev):
                if t >= 2 or has_prev:
                    act.wait_ge(turned_ready, b * TILES + t - 1)
                if has_prev and t % GT == 0:
                    act.wait_ge(rden_ready, (b - 1) * GROUPS + t // GT + 1)
                act.wait_ge(max_ready, b * TILES + t + 1)
                nc.scalar.activation(P[:, t % 2, :], ring[:, S_SLOT[t], :], ACT.Exp, bias=negmax[:, t:t + 1],
                                     accum_out=den[:, t:t + 1]).then_inc(probs_ready, 1)

            def high_turned(b, t, has_prev):
                g, k = divmod(t, GT)
                if has_prev and k == 0:
                    act.wait_ge(pieces_done, (b - 1) * PIECES * GROUPS + (g + 1) * PIECES)
                act.wait_ge(turned_ready, b * TILES + t + 1)
                nc.scalar.activation(PT_hi[:, g, :, k * TILE:(k + 1) * TILE],
                                     turned[:, :].rearrange("p (j r) -> p j r", j=TILES),
                                     ACT.Copy).then_inc(turned_hi, 1)

            def copy_rden(b, g):
                act.wait_ge(rden_spread, b * GROUPS + g + 1)
                if g > 0 or not isinstance(b, int) or b > 0:
                    act.wait_ge(scaled_ready, b * GROUPS + g)
                nc.scalar.activation(rdenB[:, :], small[:, :], ACT.Copy).then_inc(rden_copied, 1)

            act.wait_ge(w_loaded, 16 * 3)
            copy_m(0)
            copy_r(0)
            copy_a(0)
            high_t(0)
            act.wait_ge(phi_w_ready, 2)
            high_phi(0)

            def image(b, has_prev, has_next):
                for t in range(TILES):
                    if t == 0:
                        if has_prev:
                            high_turned(b - 1, 7, False)
                            copy_rden(b - 1, 0)
                    else:
                        high_turned(b, t - 1, has_prev)
                    exps(b, t, has_prev)
                    if t == 2 and has_next:
                        copy_m(b + 1)
                    if t == 3 and has_next:
                        copy_r(b + 1)
                    if t == 4:
                        if has_prev:
                            copy_rden(b - 1, 1)
                        high_v(b, has_prev)
                        if has_next:
                            act.wait_ge(z_ready, b + 1)
                            copy_a(b + 1)
                if has_next:
                    act.wait_ge(scores_ready, (b + 1) * TILES)
                    high_t(b + 1)
                    high_phi(b + 1)

            over_images(act, image)
            last = IMAGES - 1
            high_turned(last, 7, False)
            copy_rden(last, 0)
            copy_rden(last, 1)

        @block.vector
        def _(dve):
            def copy_pg(b):
                dve.wait_ge(pg_ready, b + 1)
                nc.vector.tensor_tensor(pgT[:, :, :], ring[:, PG_SLOT, :].rearrange("p (j c) -> p j c", j=TILES),
                                        pg_b[:, :].rearrange("p (a c) -> p a c", a=1).broadcast_to([C, TILES, C]),
                                        ALU.add).then_inc(pg_copied, 1)

            def make_z(b):
                dve.wait_ge(ax_ready, b + 1)
                nc.vector.scalar_tensor_tensor(out=Z[:, :], in0=ring[:, AX_SLOT, :], scalar=d[:, :], in1=X[:, :],
                                               op0=ALU.add, op1=ALU.add).then_inc(z_ready, 1)

            def low(lo, hi, slot, hi_done, bias, done, b):
                dve.wait_ge(hi_done, b + 1)
                nc.vector.scalar_tensor_tensor(out=lo[:, :], in0=ring[:, slot, :], scalar=bias,
                                               in1=hi[:, :].bitcast(F32), op0=ALU.add,
                                               op1=ALU.subtract).then_inc(done, 1)

            def low_t(b):
                low(T_lo, T_hi, T_SLOT, t_hi, w[:, B_T:B_T + 1], t_lo, b)

            def low_phi(b):
                low(Phi_lo, Phi_hi, PHI_SLOT, phi_hi, phi_b[:, :], phi_lo, b)

            def low_v(b):
                dve.wait_ge(v_hi, b + 1)
                nc.vector.tensor_tensor(V_lo[:, :, :].rearrange("p j c -> p (j c)"), ring[:, V_SLOT, :],
                                        V_hi[:, :, :].rearrange("p j c -> p (j c)").bitcast(F32),
                                        ALU.subtract).then_inc(v_lo, 1)

            def row_max(b, t):
                dve.wait_ge(scores_ready, b * TILES + t + 1)
                nc.vector.tensor_reduce(negmax[:, t:t + 1], ring[:, S_SLOT[t], :], AX.X, ALU.max,
                                        negate=True).then_inc(max_ready, 1)

            def low_turned(b, t):
                g, k = divmod(t, GT)
                dve.wait_ge(turned_hi, b * TILES + t + 1)
                nc.vector.tensor_tensor(PT_lo[:, g, :, k * TILE:(k + 1) * TILE],
                                        turned[:, :].rearrange("p (j r) -> p j r", j=TILES),
                                        PT_hi[:, g, :, k * TILE:(k + 1) * TILE].bitcast(F32),
                                        ALU.subtract).then_inc(turned_lo, 1)

            def invert(b, g):
                dve.wait_ge(probs_ready, b * TILES + (g + 1) * GT)
                nc.vector.reciprocal(rden[:, g * GT:(g + 1) * GT],
                                     den[:, g * GT:(g + 1) * GT]).then_inc(rden_ready, 1)

            def scale(b, g):
                dve.wait_ge(rden_copied, b * GROUPS + g + 1)
                dve.wait_ge(pieces_done, (b * GROUPS + g + 1) * PIECES)
                dve.wait_ge(zres_ready, b * GROUPS + g + 1)
                nc.vector.tensor_tensor(scaled[:, g, :], numer[:, :], rdenB[:, :], ALU.mult).then_inc(scaled_ready, 1)

            dve.wait_ge(w_loaded, 16 * 3)
            nc.vector.tensor_scalar(phi_w[:, :], w[:, W_P:W_P + C], float(C) ** -0.5, None,
                                    ALU.mult).then_inc(phi_w_ready, 1)
            nc.vector.tensor_scalar(phi_b[:, :], w[:, B_P:B_P + 1], float(C) ** -0.5, None,
                                    ALU.mult).then_inc(phi_w_ready, 1)
            copy_pg(0)
            dve.wait_ge(a_copied, 1)
            make_z(0)
            low_t(0)
            low_phi(0)

            def image(b, has_prev, has_next):
                if has_prev:
                    low_turned(b - 1, 7)
                    scale(b - 1, 0)
                    invert(b - 1, 1)
                row_max(b, 0)
                for t in range(1, TILES):
                    row_max(b, t)
                    low_turned(b, t - 1)
                    if t == 1 and has_next:
                        copy_pg(b + 1)
                    if t == 4:
                        if has_prev:
                            scale(b - 1, 1)
                        invert(b, 0)
                        low_v(b)
                    if t == 5 and has_next:
                        dve.wait_ge(zres_ready, (b + 1) * GROUPS)
                        dve.wait_ge(a_copied, b + 2)
                        make_z(b + 1)
                if has_next:
                    low_t(b + 1)
                    low_phi(b + 1)

            over_images(dve, image)
            last = IMAGES - 1
            low_turned(last, 7)
            invert(last, 1)
            scale(last, 0)
            scale(last, 1)

        @block.gpsimd
        def _(pool):
            nc.gpsimd.memset(MT[:, CI:C], 0.0).then_inc(pad_ready, 1)
            nc.gpsimd.memset(identity[:, :], 0.0).then_inc(identity_ready, 1)
            pool.wait_ge(identity_ready, 1)
            nc.gpsimd.affine_select(out=identity[:, :], in_=identity[:, :], compare_op=ALU.not_equal, fill=1.0,
                                    base=0, pattern=[[-1, C]], channel_multiplier=1).then_inc(identity_ready, 1)

            def residual(b, g):
                cols = slice(g * BANK, (g + 1) * BANK)
                nc.gpsimd.tensor_tensor(Zres[:, cols], Z[:, cols], w[:, B_C:B_C + 1].broadcast_to([C, BANK]),
                                        ALU.add).then_inc(zres_ready, 1)

            def finish(b, g, first=False):
                pool.wait_ge(scaled_ready, b * GROUPS + g + 1)
                pool.wait_ge(zres_ready, b * GROUPS + g + 1)
                if not first:
                    pool.wait_ge(stored[g], b * 16)
                nc.gpsimd.tensor_tensor(result[:, g, :], scaled[:, g, :], Zres[:, g * BANK:(g + 1) * BANK],
                                        ALU.add).then_inc(result_ready, 1)

            pool.wait_ge(w_loaded, 16 * 3)
            pool.wait_ge(z_ready, 1)
            for g in range(GROUPS):
                residual(0, g)

            def image(b, first=False):
                pool.wait_ge(z_ready, b + 1)
                for g in range(GROUPS):
                    finish(b - 1, g, first)
                    pool.wait_ge(result_ready, (b - 1) * GROUPS + g + 1)
                    residual(b, g)

            image(1, first=True)
            with pool.Fori(2, IMAGES) as b:
                image(b)
            for g in range(GROUPS):
                finish(IMAGES - 1, g)


def kernel(x, L0_conv_g_w, L0_conv_g_b, L0_conv_theta_w, L0_conv_theta_b, L0_conv_phi_w, L0_conv_phi_b,
           L0_conv_out_w, L0_conv_out_b, L1_conv_theta_w, L1_conv_theta_b, L1_conv_phi_w, L1_conv_phi_b,
           L1_conv_conv1_w, L1_conv_conv1_b):
    import numpy as np
    import concourse.bacc as bacc
    from concourse.bass_utils import run_bass_kernel_spmd

    n, c, h, wd = x.shape
    arrays = {
        "x_dram": np.ascontiguousarray(x.reshape(n, c, h * wd)),
        "weights_dram": np.concatenate(
            [L0_conv_phi_w.T, L0_conv_g_w.T, L1_conv_theta_w.T, L1_conv_phi_w.T, L1_conv_conv1_w.T,
             L1_conv_theta_b[:, None], L1_conv_phi_b[:, None], L1_conv_conv1_b[:, None],
             L0_conv_out_b[:, None]], axis=1),
        "inner_dram": np.concatenate([L0_conv_theta_w, L0_conv_out_w.T, L0_conv_theta_b[:, None]], axis=1),
        "pg_bias_dram": np.concatenate([L0_conv_phi_b, L0_conv_g_b])[None, :],
    }
    nc = bacc.Bacc("TRN2", target_bir_lowering=False, num_devices=1)
    args = [nc.dram_tensor(name, a.shape, mybir.dt.from_np(a.dtype), kind="ExternalInput").ap()
            for name, a in arrays.items()]
    args.append(nc.dram_tensor("out_dram", (n, c, h * wd), F32, kind="ExternalOutput").ap())
    build(nc, *args)
    r = run_bass_kernel_spmd(nc, [arrays], core_ids=[0])
    return r.results[0]["out_dram"].reshape(n, c, h, wd)
```

```python
from contextlib import ExitStack

import concourse.bass as bass
from concourse import mybir

F32 = mybir.dt.float32
F32R = mybir.dt.float32r
BF16 = mybir.dt.bfloat16
ALU = mybir.AluOpType
ACT = mybir.ActivationFunctionType
AX = mybir.AxisListType

IMAGES = 4
C = 128
CI = 64
PIX = 1024
TILE = 128
TILES = PIX // TILE
BANK = 512
GROUPS = PIX // BANK
GT = TILES // GROUPS
PIECES = 4
CHUNKS_PER_PIECE = TILES // PIECES
HALVES = PIX // BANK
CHUNKS_PER_HALF = TILES // HALVES
PIECES_PER_HALF = PIECES // HALVES

LAST_COLS = BANK - TILE
LAST_EARLY = 5

W_T, W_P, W_C = 0, C, 2 * C
B_T, B_P, B_C, B_O = 3 * C, 3 * C + 1, 3 * C + 2, 3 * C + 3
W_COLS = 3 * C + 4
I_T, I_O, I_TB = 0, C, 2 * C
I_COLS = 2 * C + 1


WARM_UP = 28


def build(nc, x, pg_weights, pg_bias, inner, weights, out):
    with ExitStack() as ctx:
        def sb(name, shape, dt=F32):
            return ctx.enter_context(nc.sbuf_tensor(name, shape, dt))

        def sem(name):
            return ctx.enter_context(nc.semaphore(name))

        pg_w = sb("pg_w", [C, C])
        w = sb("w", [C, W_COLS])
        wi = sb("wi", [CI, I_COLS])
        pg_b = sb("pg_b", [C, C])
        phi_w = sb("phi_w", [C, C])
        phi_b = sb("phi_b", [C, 1])
        T_w_hi, T_w_lo = sb("T_w_hi", [C, C], F32R), sb("T_w_lo", [C, C], F32R)
        phi_w_hi, phi_w_lo = sb("phi_w_hi", [C, C], F32R), sb("phi_w_lo", [C, C], F32R)
        identity = sb("identity", [C, C])
        table = sb("table", [C, 1])
        idle = sb("idle", [C, C], BF16)
        X_first = sb("X_first", [C, PIX])
        X = sb("X", [C, PIX])
        X_hi, X_lo = sb("X_hi", [C, PIX], F32R), sb("X_lo", [C, PIX], F32R)
        pgT = sb("pgT", [C, TILES, C])
        MT = sb("MT", [CI, C])
        R = sb("R", [CI, C])
        AT = sb("AT", [C, C])
        AT_hi, AT_lo = sb("AT_hi", [C, C], F32R), sb("AT_lo", [C, C], F32R)
        d = sb("d", [C, 1])
        Z = sb("Z", [C, PIX])
        Z_hi, Z_lo = sb("Z_hi", [C, PIX], F32R), sb("Z_lo", [C, PIX], F32R)
        Zres = sb("Zres", [C, PIX])
        T_hi, T_lo = sb("T_hi", [C, PIX], F32R), sb("T_lo", [C, PIX], F32R)
        Phi_hi, Phi_lo = sb("Phi_hi", [C, PIX], F32R), sb("Phi_lo", [C, PIX], F32R)
        V_hi, V_lo = sb("V_hi", [C, TILES * C], F32R), sb("V_lo", [C, TILES * C], F32R)
        negmax = sb("negmax", [C, TILES])
        den = sb("den", [C, TILES])
        rden = sb("rden", [C, TILES])
        P = sb("P", [C, 2, PIX])
        PT_hi = sb("PT_hi", [C, GROUPS, TILES, BANK], F32R)
        PT_lo = sb("PT_lo", [C, GROUPS, TILES, BANK], F32R)
        attended = sb("attended", [C, GROUPS, BANK])
        result = sb("result", [C, GROUPS, BANK])

        ring = ctx.enter_context(nc.psum_tensor("ring", [C, 2, PIX], F32))
        turned = ctx.enter_context(nc.psum_tensor("turned", [C, PIX], F32))
        numer = ctx.enter_context(nc.psum_tensor("numer", [C, BANK], F32))
        small = ctx.enter_context(nc.psum_tensor("small", [C, BANK], F32))

        last_rows = small[:, 0:LAST_COLS]
        last_tile = ring[:, 0, 0:TILE]

        S_SLOT = [1, 0, 1, 1, 0, 0, 0, 1]
        PG_SLOT, M_SLOT, V_SLOT, AX_SLOT, T_SLOT, PHI_SLOT = 0, 0, 1, 1, 0, 1

        pg_w_loaded, pg_b_loaded, wi_loaded, w_loaded = (
            sem(n + "_loaded") for n in ("pg_w", "pg_b", "wi", "w"))
        first_loaded = [sem(f"first_loaded{h}") for h in range(HALVES)]
        x_loaded = sem("x_loaded")
        idle_ready = sem("idle_ready")
        identity_ready, pad_ready, table_ready = sem("identity_ready"), sem("pad_ready"), sem("table_ready")
        phi_w_ready, w_hi, w_lo = sem("phi_w_ready"), sem("w_hi"), sem("w_lo")
        pg_ready, pg_copied = sem("pg_ready"), sem("pg_copied")
        m_ready, m_copied = sem("m_ready"), sem("m_copied")
        r_ready, r_copied = sem("r_ready"), sem("r_copied")
        a_ready, a_copied = sem("a_ready"), sem("a_copied")
        x_hi, x_lo, a_lo, z_hi, z_lo = (sem(n) for n in ("x_hi", "x_lo", "a_lo", "z_hi", "z_lo"))
        ax_ready, t_ready, t_hi, phi_ready, phi_hi = (
            sem(n) for n in ("ax_ready", "t_ready", "t_hi", "phi_ready", "phi_hi"))
        z_ready, zres_ready, t_lo, phi_lo = sem("z_ready"), sem("zres_ready"), sem("t_lo"), sem("phi_lo")
        half = {n: sem("half_" + n) for n in ("pg", "pg_copied", "next_pg", "next_copied", "ax", "z", "t", "t_hi", "t_lo", "phi", "phi_hi", "phi_lo")}
        v_ready, v_hi, v_lo = sem("v_ready"), sem("v_hi"), sem("v_lo")
        scores_ready, max_ready, probs_ready = sem("scores_ready"), sem("max_ready"), sem("probs_ready")
        rden_ready, probs_normed = sem("rden_ready"), sem("probs_normed")
        turned_ready, turned_hi, turned_lo = sem("turned_ready"), sem("turned_hi"), sem("turned_lo")
        pieces_done, numer_copied, result_ready = sem("pieces_done"), sem("numer_copied"), sem("result_ready")
        stored = [sem(f"stored{g}") for g in range(GROUPS)]
        last_stored = sem("last_stored")

        block = ctx.enter_context(nc.Block())

        def columns(h):
            return slice(h * BANK, (h + 1) * BANK)

        def half_chunks(h):
            return slice(h * CHUNKS_PER_HALF, (h + 1) * CHUNKS_PER_HALF)

        def half_range(h):
            return range(h * CHUNKS_PER_HALF, (h + 1) * CHUNKS_PER_HALF)

        def over_images(eng, first_image, image):
            first_image()
            with eng.Fori(1, IMAGES - 1) as b:
                image(b, True)
            image(IMAGES - 1, False)

        @block.sync
        def _(sp):
            for h in range(HALVES):
                sp.dma_start(X_first[:, columns(h)], x[0, :, columns(h)]).then_inc(first_loaded[h], 16)
            sp.dma_start(wi[:, :], inner).then_inc(wi_loaded, 16)
            sp.dma_start(X[:, :], x[1]).then_inc(x_loaded, 16)

            def load(b):
                sp.wait_ge(z_ready, b)
                sp.dma_start(X[:, :], x[b]).then_inc(x_loaded, 16)

            def store(b):
                for g in range(GROUPS):
                    sp.wait_ge(result_ready, b * GROUPS + g + 1)
                    sp.dma_start(out[b, :, columns(g)], result[:, g, :]).then_inc(stored[g], 16)

            with sp.Fori(0, IMAGES - 2) as b:
                load(b + 2)
                store(b)
            store(IMAGES - 2)
            parts = ((0, slice(0, BANK)), (1, slice(0, LAST_COLS)), (1, slice(LAST_COLS, BANK)))
            for n, (g, cols) in enumerate(parts):
                sp.wait_ge(result_ready, (IMAGES - 1) * GROUPS + n + 1)
                sp.dma_start(out[IMAGES - 1, :, g * BANK + cols.start:g * BANK + cols.stop],
                             result[:, g, cols]).then_inc(last_stored, 16)
            for g in range(GROUPS):
                sp.wait_ge(stored[g], 16 * (IMAGES - 1))
            sp.wait_ge(last_stored, 16 * len(parts))

        @block.tensor
        def _(pe):
            def phi_g_chunks(to, source, chunks):
                for j in chunks:
                    mm = nc.tensor.matmul(to[:, j * C:(j + 1) * C], source[:, j * TILE:(j + 1) * TILE],
                                          pg_w[:, :], start=True, stop=True)
                return mm

            def phi_g(b):
                pe.wait_ge(x_loaded, b * 16)
                phi_g_chunks(ring[:, PG_SLOT, :], X, range(TILES)).then_inc(pg_ready, 1)

            def inner_chunks(chunks):
                for j in chunks:
                    mm = nc.tensor.matmul(ring[0:CI, M_SLOT, 0:CI], pgT[:, j, CI:C], pgT[:, j, 0:CI],
                                          start=(j == 0), stop=(j == TILES - 1))
                return mm

            def inner_product(b):
                pe.wait_ge(pg_copied, b + 1)
                inner_chunks(range(TILES)).then_inc(m_ready, 1)

            def out_times_inner(b):
                pe.wait_ge(m_copied, b + 1)
                nc.tensor.matmul(small[:, 0:C], MT[:, :], wi[:, I_O:I_O + C],
                                 start=True, stop=True).then_inc(r_ready, 1)

            def fold(b):
                pe.wait_ge(r_copied, b + 1)
                nc.tensor.matmul(small[:, 0:C], wi[:, I_T:I_T + C], R[:, :], start=True, stop=False)
                nc.tensor.matmul(small[:, 0:C], identity[:, :], identity[:, :], start=False, stop=True)
                nc.tensor.matmul(small[:, C:C + 1], R[:, :], wi[:, I_TB:I_TB + 1],
                                 start=True, stop=True).then_inc(a_ready, 1)

            def conv_half(slot, weight, source, h, done):
                nc.tensor.matmul(ring[:, slot, columns(h)], weight, source[:, columns(h)],
                                 start=True, stop=True).then_inc(done, 1)

            def three_passes(slot, lefts, rights, done):
                (left_hi, left_lo), (right_hi, right_lo) = lefts, rights
                for n, (left, right) in enumerate(((left_hi, right_hi), (left_hi, right_lo), (left_lo, right_hi))):
                    for h in range(GROUPS):
                        mm = nc.tensor.matmul(ring[:, slot, columns(h)], left, right[:, columns(h)],
                                              start=(n == 0), stop=(n == 2))
                mm.then_inc(done, 1)

            def values(b):
                pe.wait_ge(probs_ready, b * TILES + 4)
                for j in range(TILES):
                    mm = nc.tensor.matmul(ring[:, V_SLOT, j * C:(j + 1) * C], Z[:, j * TILE:(j + 1) * TILE],
                                          w[:, W_C:W_C + C], start=True, stop=True)
                mm.then_inc(v_ready, 1)

            def fold_x(b):
                pe.wait_ge(x_lo, b)
                pe.wait_ge(a_lo, b)
                pe.wait_ge(v_lo, b)
                three_passes(AX_SLOT, (AT_hi[:, :], AT_lo[:, :]), (X_hi, X_lo), ax_ready)

            def theta(b):
                pe.wait_ge(w_lo, 2)
                pe.wait_ge(z_lo, b)
                pe.wait_ge(probs_ready, (b - 1) * TILES + 7)
                three_passes(T_SLOT, (T_w_hi[:, :], T_w_lo[:, :]), (Z_hi, Z_lo), t_ready)

            def phi(b):
                pe.wait_ge(probs_ready, b * TILES)
                three_passes(PHI_SLOT, (phi_w_hi[:, :], phi_w_lo[:, :]), (Z_hi, Z_lo), phi_ready)

            def scores_half(t, h):
                rows = slice(t * TILE, (t + 1) * TILE)
                for n, (left, right) in enumerate(((T_hi, Phi_hi), (T_hi, Phi_lo), (T_lo, Phi_hi))):
                    mm = nc.tensor.matmul(ring[:, S_SLOT[t], columns(h)], left[:, rows], right[:, columns(h)],
                                          start=(n == 0), stop=(n == 2))
                return mm

            def scores(t):
                rows = slice(t * TILE, (t + 1) * TILE)
                three_passes(S_SLOT[t], (T_hi[:, rows], T_lo[:, rows]), (Phi_hi, Phi_lo), scores_ready)

            def turn(b, t, h, first=False):
                if h == 0:
                    pe.wait_ge(probs_normed, b * TILES + t + 1)
                if not first:
                    pe.wait_ge(turned_lo, (b * TILES + t - 1) * HALVES + h + 1)
                for j in half_range(h):
                    mm = nc.tensor.transpose(turned[:, j * TILE:(j + 1) * TILE],
                                             P[:, t % 2, j * TILE:(j + 1) * TILE], identity[:, :])
                mm.then_inc(turned_ready, 1)

            def turn_tile(b, t, first=False):
                for h in range(HALVES):
                    turn(b, t, h, first)

            def attend_last(to, rows, j):
                chunk = slice(j * C, (j + 1) * C)
                for n, (left, right) in enumerate(((V_hi, PT_hi), (V_hi, PT_lo), (V_lo, PT_hi))):
                    mm = nc.tensor.matmul(to, left[:, chunk], right[:, GROUPS - 1, j, rows],
                                          start=(j == 0 and n == 0), stop=(j == TILES - 1 and n == 2))
                return mm

            def attend(b, g, i, first=False):
                if i % PIECES_PER_HALF == 0:
                    h = i // PIECES_PER_HALF
                    pe.wait_ge(turned_lo, (b * TILES + (g + 1) * GT - 1) * HALVES + h + 1)
                if i == 0:
                    if g == 0:
                        pe.wait_ge(v_lo, b + 1)
                    if not first:
                        pe.wait_ge(numer_copied, b * GROUPS + g)
                for j in range(i * CHUNKS_PER_PIECE, (i + 1) * CHUNKS_PER_PIECE):
                    chunk = slice(j * C, (j + 1) * C)
                    for n, (left, right) in enumerate(((V_hi, PT_hi), (V_hi, PT_lo), (V_lo, PT_hi))):
                        mm = nc.tensor.matmul(numer[:, :], left[:, chunk], right[:, g, j, :],
                                              start=(j == 0 and n == 0), stop=(j == TILES - 1 and n == 2))
                mm.then_inc(pieces_done, 1)

            pe.wait_ge(idle_ready, 1)
            for _ in range(WARM_UP):
                nc.tensor.matmul(small[:, 0:C], idle[:, :], idle[:, :], start=True, stop=True)
            pe.wait_ge(pg_w_loaded, 16)
            for h in range(HALVES):
                pe.wait_ge(first_loaded[h], 16)
                phi_g_chunks(ring[:, PG_SLOT, :], X_first, half_range(h)).then_inc(half["pg"] if h == 0 else pg_ready, 1)
            for h in range(HALVES):
                pe.wait_ge(half["pg_copied"] if h == 0 else pg_copied, 1)
                mm = inner_chunks(half_range(h))
            mm.then_inc(m_ready, 1)
            pe.wait_ge(x_loaded, 16)
            phi_g_chunks(turned, X, range(0, 2))
            pe.wait_ge(pad_ready, 1)
            pe.wait_ge(identity_ready, 2)
            pe.wait_ge(wi_loaded, 16)
            out_times_inner(0)
            phi_g_chunks(turned, X, range(2, 4)).then_inc(half["next_pg"], 1)
            fold(0)
            phi_g_chunks(turned, X, range(4, TILES)).then_inc(pg_ready, 1)
            pe.wait_ge(a_copied, 1)
            for h in range(HALVES):
                conv_half(AX_SLOT, AT[:, :], X_first, h, half["ax"])
            pe.wait_ge(phi_w_ready, 2)
            pe.wait_ge(half["z"], 1)
            conv_half(T_SLOT, w[:, W_T:W_T + C], Z, 0, half["t"])
            pe.wait_ge(z_ready, 1)
            conv_half(PHI_SLOT, phi_w[:, :], Z, 0, half["phi"])
            conv_half(PHI_SLOT, phi_w[:, :], Z, 1, half["phi"])
            conv_half(T_SLOT, w[:, W_T:W_T + C], Z, 1, half["t"])

            def first_image():
                for h in range(HALVES):
                    pe.wait_ge(half["phi_lo"] if h == 0 else phi_lo, 1)
                    pe.wait_ge(half["t_lo"], 1)
                    mm = scores_half(0, h)
                mm.then_inc(scores_ready, 1)
                pe.wait_ge(t_lo, 1)
                scores(1)
                pe.wait_ge(probs_ready, 1)
                scores(2)
                pe.wait_ge(pg_copied, 2)
                turn_tile(0, 0, first=True)
                pe.wait_ge(probs_ready, 2)
                inner_product(1)
                pe.wait_ge(probs_ready, 3)
                scores(3)
                turn_tile(0, 1)
                pe.wait_ge(a_copied, 1)
                out_times_inner(1)
                scores(4)
                turn_tile(0, 2)
                values(0)
                fold(1)
                pe.wait_ge(probs_ready, 5)
                scores(5)
                turn_tile(0, 3)
                fold_x(1)
                pe.wait_ge(probs_ready, 6)
                scores(6)
                turn(0, 4, 0)
                attend(0, 0, 0, first=True)
                turn(0, 4, 1)
                pe.wait_ge(z_ready, 2)
                scores(7)
                turn(0, 5, 0)
                attend(0, 0, 1)
                turn(0, 5, 1)
                theta(1)
                turn(0, 6, 0)
                attend(0, 0, 2)
                turn(0, 6, 1)
                phi(1)
                attend(0, 0, 3)

            def image(b, has_next):
                pe.wait_ge(t_lo, b + 1)
                if has_next:
                    phi_g(b + 1)
                pe.wait_ge(phi_lo, b + 1)
                scores(0)
                turn_tile(b - 1, 7)
                if has_next:
                    pe.wait_ge(pg_copied, b + 2)
                scores(1)
                attend(b - 1, 1, 0)
                turn(b, 0, 0)
                attend(b - 1, 1, 1)
                turn(b, 0, 1)
                scores(2)
                turn(b, 1, 0)
                attend(b - 1, 1, 2)
                turn(b, 1, 1)
                if has_next:
                    inner_product(b + 1)
                pe.wait_ge(probs_ready, b * TILES + 3)
                scores(3)
                turn(b, 2, 0)
                attend(b - 1, 1, 3)
                turn(b, 2, 1)
                if has_next:
                    pe.wait_ge(a_copied, b + 1)
                    out_times_inner(b + 1)
                scores(4)
                turn(b, 3, 0)
                values(b)
                turn(b, 3, 1)
                if has_next:
                    fold(b + 1)
                pe.wait_ge(probs_ready, b * TILES + 5)
                scores(5)
                turn(b, 4, 0)
                attend(b, 0, 0)
                turn(b, 4, 1)
                if has_next:
                    fold_x(b + 1)
                pe.wait_ge(probs_ready, b * TILES + 6)
                scores(6)
                turn(b, 5, 0)
                attend(b, 0, 1)
                turn(b, 5, 1)
                if has_next:
                    pe.wait_ge(z_ready, b + 2)
                else:
                    pe.wait_ge(v_lo, b + 1)
                scores(7)
                turn(b, 6, 0)
                if has_next:
                    theta(b + 1)
                attend(b, 0, 2)
                turn(b, 6, 1)
                if has_next:
                    phi(b + 1)
                attend(b, 0, 3)

            over_images(pe, first_image, image)
            pe.wait_ge(turned_lo, (IMAGES * TILES - 1) * HALVES)
            for j in range(LAST_EARLY):
                attend_last(last_rows, slice(0, LAST_COLS), j)
            for h in range(HALVES):
                turn(IMAGES - 1, 7, h)
            for j in range(LAST_EARLY, TILES):
                mm = attend_last(last_rows, slice(0, LAST_COLS), j)
            mm.then_inc(pieces_done, 1)
            for h in range(HALVES):
                pe.wait_ge(turned_lo, (IMAGES * TILES - 1) * HALVES + h + 1)
                for j in half_range(h):
                    mm = attend_last(last_tile, slice(LAST_COLS, BANK), j)
            mm.then_inc(pieces_done, 1)

        @block.scalar
        def _(act):
            act.dma_start(pg_w[:, :], pg_weights).then_inc(pg_w_loaded, 16)
            act.dma_start(pg_b[:, :], pg_bias.broadcast_to([C, C])).then_inc(pg_b_loaded, 16)
            act.dma_start(w[:, :], weights).then_inc(w_loaded, 16)
            act.wait_ge(table_ready, 1)
            nc.scalar.activation(table[:, :], table[:, :], ACT.Exp)

            def copy_m(b):
                act.wait_ge(m_ready, b + 1)
                nc.scalar.activation(MT[:, 0:CI], ring[0:CI, M_SLOT, 0:CI], ACT.Copy,
                                     scale=1.0 / PIX).then_inc(m_copied, 1)

            def copy_r(b):
                act.wait_ge(r_ready, b + 1)
                nc.scalar.activation(R[:, :], small[0:CI, 0:C], ACT.Copy).then_inc(r_copied, 1)

            def copy_a(b, to):
                act.wait_ge(a_ready, b + 1)
                nc.scalar.activation(d[:, :], small[:, C:C + 1], ACT.Identity, bias=w[:, B_O:B_O + 1])
                nc.scalar.activation(to[:, :], small[:, 0:C], ACT.Copy).then_inc(a_copied, 1)

            def high_x(b, first):
                act.wait_ge(x_loaded, b * 16)
                if not first:
                    act.wait_ge(ax_ready, b - 1)
                nc.scalar.activation(X_hi[:, :], X[:, :], ACT.Copy).then_inc(x_hi, 1)

            def make_z(b, first):
                act.wait_ge(zres_ready, b * GROUPS)
                act.wait_ge(v_ready, b)
                if not first:
                    act.wait_ge(z_lo, b - 1)
                act.wait_ge(ax_ready, b)
                nc.scalar.activation(Z[:, :], ring[:, AX_SLOT, :], ACT.Identity, bias=d[:, :]).then_inc(z_ready, 1)

            def high_z(b, first):
                act.wait_ge(z_ready, b + 1)
                if not first:
                    act.wait_ge(phi_ready, b - 1)
                nc.scalar.activation(Z_hi[:, :], Z[:, :], ACT.Copy).then_inc(z_hi, 1)

            def high(hi, slot, bias, cols, done):
                nc.scalar.activation(hi[:, cols], ring[:, slot, cols], ACT.Identity, bias=bias).then_inc(done, 1)

            def high_t(b):
                act.wait_ge(t_ready, b)
                act.wait_ge(scores_ready, b * TILES)
                high(T_hi, T_SLOT, w[:, B_T:B_T + 1], slice(0, PIX), t_hi)

            def high_phi(b):
                act.wait_ge(phi_ready, b)
                high(Phi_hi, PHI_SLOT, phi_b[:, :], slice(0, PIX), phi_hi)

            def high_v(b, has_prev):
                if has_prev:
                    act.wait_ge(pieces_done, b * PIECES * GROUPS)
                act.wait_ge(v_ready, b + 1)
                nc.scalar.activation(V_hi[:, :], ring[:, V_SLOT, :], ACT.Copy).then_inc(v_hi, 1)

            def exps(b, t, has_prev):
                if t >= 2 or has_prev:
                    act.wait_ge(turned_ready, (b * TILES + t - 1) * HALVES)
                act.wait_ge(max_ready, b * TILES + t + 1)
                nc.scalar.activation(P[:, t % 2, :], ring[:, S_SLOT[t], :], ACT.Exp, bias=negmax[:, t:t + 1],
                                     accum_out=den[:, t:t + 1]).then_inc(probs_ready, 1)

            def high_turned(b, t, h, has_prev=False):
                g, k = divmod(t, GT)
                if has_prev and k == 0 and h == 0:
                    act.wait_ge(pieces_done, (b - 1) * PIECES * GROUPS + (g + 1) * PIECES)
                act.wait_ge(turned_ready, (b * TILES + t) * HALVES + h + 1)
                nc.scalar.activation(PT_hi[:, g, half_chunks(h), k * TILE:(k + 1) * TILE],
                                     turned[:, columns(h)].rearrange("p (j r) -> p j r", j=CHUNKS_PER_HALF),
                                     ACT.Copy).then_inc(turned_hi, 1)

            def copy_numer(b, g):
                act.wait_ge(pieces_done, (b * GROUPS + g + 1) * PIECES)
                act.wait_ge(zres_ready, b * GROUPS + g + 1)
                nc.scalar.activation(attended[:, g, :], numer[:, :], ACT.Copy).then_inc(numer_copied, 1)

            def high_t_half(h):
                act.wait_ge(half["t"], h + 1)
                high(T_hi, T_SLOT, w[:, B_T:B_T + 1], columns(h), half["t_hi"])

            def high_phi_half(h):
                act.wait_ge(half["phi"], h + 1)
                high(Phi_hi, PHI_SLOT, phi_b[:, :], columns(h), half["phi_hi"])

            act.wait_ge(w_loaded, 16)
            nc.scalar.activation(T_w_hi[:, :], w[:, W_T:W_T + C], ACT.Copy).then_inc(w_hi, 1)
            copy_m(0)
            copy_r(0)
            copy_a(0, AT)
            high_x(1, first=True)
            act.wait_ge(phi_w_ready, 2)
            nc.scalar.activation(phi_w_hi[:, :], phi_w[:, :], ACT.Copy).then_inc(w_hi, 1)
            high_t_half(0)
            high_phi_half(0)
            high_phi_half(1)
            high_t_half(1)

            def first_image():
                exps(0, 0, False)
                for t in range(1, TILES):
                    exps(0, t, False)
                    if t == 2:
                        copy_m(1)
                    if t == 3:
                        copy_r(1)
                    if t == 4:
                        high_v(0, False)
                        copy_a(1, AT_hi)
                    if t == 5:
                        make_z(1, first=True)
                    high_turned(0, t - 1, 0)
                    if t == 7:
                        high_t(1)
                    high_turned(0, t - 1, 1)
                    if t == 5:
                        high_z(1, first=True)
                    if t == 7:
                        high_phi(1)
                copy_numer(0, 0)

            def image(b, has_next):
                high_turned(b - 1, 7, 0)
                exps(b, 0, True)
                high_turned(b - 1, 7, 1)
                for t in range(1, TILES):
                    high_turned(b, t - 1, 0, True)
                    exps(b, t, True)
                    if t == 4:
                        high_v(b, True)
                    if t == 7 and has_next:
                        high_t(b + 1)
                    high_turned(b, t - 1, 1)
                    if t == 3:
                        copy_numer(b - 1, 1)
                    if not has_next:
                        continue
                    if t == 2:
                        copy_m(b + 1)
                    if t == 3:
                        copy_r(b + 1)
                        high_x(b + 1, first=False)
                    if t == 4:
                        act.wait_ge(z_ready, b + 1)
                        copy_a(b + 1, AT_hi)
                    if t == 5:
                        make_z(b + 1, first=False)
                        high_z(b + 1, first=False)
                    if t == 7:
                        high_phi(b + 1)
                if has_next:
                    copy_numer(b, 0)

            over_images(act, first_image, image)
            for h in range(HALVES):
                high_turned(IMAGES - 1, 7, h)

        @block.vector
        def _(dve):
            nc.vector.memset(idle[:, :], 0.0).then_inc(idle_ready, 1)
            nc.vector.memset(table[:, :], 0.0).then_inc(table_ready, 1)

            def copy_pg_chunks(source, chunks, count, done):
                nc.vector.tensor_tensor(pgT[:, chunks, :], source.rearrange("p (j c) -> p j c", j=count),
                                        pg_b[:, :].rearrange("p (a c) -> p a c", a=1).broadcast_to([C, count, C]),
                                        ALU.add).then_inc(done, 1)

            def copy_pg(b):
                dve.wait_ge(pg_ready, b + 1)
                copy_pg_chunks(ring[:, PG_SLOT, :], slice(0, TILES), TILES, pg_copied)

            def low_a(b):
                dve.wait_ge(a_copied, b + 1)
                nc.vector.tensor_tensor(AT_lo[:, :], small[:, 0:C], AT_hi[:, :].bitcast(F32),
                                        ALU.subtract).then_inc(a_lo, 1)

            def low(lo, hi, slot, bias, cols, done):
                nc.vector.scalar_tensor_tensor(out=lo[:, cols], in0=ring[:, slot, cols], scalar=bias,
                                               in1=hi[:, cols].bitcast(F32), op0=ALU.add,
                                               op1=ALU.subtract).then_inc(done, 1)

            def low_t(b):
                dve.wait_ge(t_hi, b)
                low(T_lo, T_hi, T_SLOT, w[:, B_T:B_T + 1], slice(0, PIX), t_lo)

            def low_phi(b):
                dve.wait_ge(phi_hi, b)
                low(Phi_lo, Phi_hi, PHI_SLOT, phi_b[:, :], slice(0, PIX), phi_lo)

            def low_v(b):
                dve.wait_ge(v_hi, b + 1)
                nc.vector.tensor_tensor(V_lo[:, :], ring[:, V_SLOT, :], V_hi[:, :].bitcast(F32),
                                        ALU.subtract).then_inc(v_lo, 1)

            def row_max(b, t):
                dve.wait_ge(scores_ready, b * TILES + t + 1)
                nc.vector.tensor_reduce(negmax[:, t:t + 1], ring[:, S_SLOT[t], :], AX.X, ALU.max,
                                        negate=True).then_inc(max_ready, 1)

            def norm(b, t):
                dve.wait_ge(probs_ready, b * TILES + t + 1)
                nc.vector.reciprocal(rden[:, t:t + 1], den[:, t:t + 1]).then_inc(rden_ready, 1)
                dve.wait_ge(rden_ready, b * TILES + t + 1)
                nc.vector.tensor_scalar(P[:, t % 2, :], P[:, t % 2, :], rden[:, t:t + 1], None,
                                        ALU.mult).then_inc(probs_normed, 1)

            def low_turned(b, t, h):
                g, k = divmod(t, GT)
                rows = slice(k * TILE, (k + 1) * TILE)
                dve.wait_ge(turned_hi, (b * TILES + t) * HALVES + h + 1)
                nc.vector.tensor_tensor(PT_lo[:, g, half_chunks(h), rows],
                                        turned[:, columns(h)].rearrange("p (j r) -> p j r", j=CHUNKS_PER_HALF),
                                        PT_hi[:, g, half_chunks(h), rows].bitcast(F32),
                                        ALU.subtract).then_inc(turned_lo, 1)

            def finish_last_group(source, g, cols, count):
                dve.wait_ge(pieces_done, (IMAGES - 1) * GROUPS * PIECES + count)
                dve.wait_ge(zres_ready, IMAGES * GROUPS)
                nc.vector.tensor_tensor(result[:, g, cols], source, Zres[:, g * BANK + cols.start:g * BANK + cols.stop],
                                        ALU.add).then_inc(result_ready, 1)

            def low_t_half(h):
                dve.wait_ge(half["t_hi"], h + 1)
                low(T_lo, T_hi, T_SLOT, w[:, B_T:B_T + 1], columns(h), t_lo if h else half["t_lo"])

            def low_phi_half(h):
                dve.wait_ge(half["phi_hi"], h + 1)
                low(Phi_lo, Phi_hi, PHI_SLOT, phi_b[:, :], columns(h), phi_lo if h else half["phi_lo"])

            dve.wait_ge(pg_b_loaded, 16)
            for h in range(HALVES):
                dve.wait_ge(half["pg"] if h == 0 else pg_ready, 1)
                copy_pg_chunks(ring[:, PG_SLOT, columns(h)], half_chunks(h), CHUNKS_PER_HALF,
                               half["pg_copied"] if h == 0 else pg_copied)
            dve.wait_ge(m_ready, 1)
            dve.wait_ge(half["next_pg"], 1)
            copy_pg_chunks(turned[:, columns(0)], half_chunks(0), CHUNKS_PER_HALF, half["next_copied"])
            dve.wait_ge(a_copied, 1)
            for h in range(HALVES):
                dve.wait_ge(half["ax"], h + 1)
                nc.vector.tensor_scalar(Z[:, columns(h)], ring[:, AX_SLOT, columns(h)], d[:, :], None,
                                        ALU.add).then_inc(z_ready if h else half["z"], 1)
            dve.wait_ge(pg_ready, 2)
            copy_pg_chunks(turned[:, columns(1)], half_chunks(1), CHUNKS_PER_HALF, pg_copied)
            low_t_half(0)
            low_phi_half(0)
            low_phi_half(1)
            low_t_half(1)

            def first_image():
                row_max(0, 0)
                for t in range(TILES):
                    if t < TILES - 1:
                        row_max(0, t + 1)
                    norm(0, t)
                    if t >= 1:
                        low_turned(0, t - 1, 0)
                    if t == 7:
                        low_t(1)
                    if t >= 1:
                        low_turned(0, t - 1, 1)
                    if t == 3:
                        low_v(0)
                        low_a(1)
                low_phi(1)

            def image(b, has_next):
                if has_next:
                    copy_pg(b + 1)
                row_max(b, 0)
                low_turned(b - 1, 7, 0)
                norm(b, 0)
                low_turned(b - 1, 7, 1)
                for t in range(1, TILES):
                    row_max(b, t)
                    low_turned(b, t - 1, 0)
                    norm(b, t)
                    if t == 4:
                        low_v(b)
                    if t == 7 and has_next:
                        low_t(b + 1)
                    low_turned(b, t - 1, 1)
                    if not has_next:
                        continue
                    if t == 4:
                        low_a(b + 1)
                    if t == 7:
                        low_phi(b + 1)

            over_images(dve, first_image, image)
            finish_last_group(numer[:, :], 0, slice(0, BANK), PIECES)
            low_turned(IMAGES - 1, 7, 0)
            low_turned(IMAGES - 1, 7, 1)
            finish_last_group(last_rows, 1, slice(0, LAST_COLS), PIECES + 1)
            finish_last_group(last_tile, 1, slice(LAST_COLS, BANK), PIECES + 2)

        @block.gpsimd
        def _(pool):
            nc.gpsimd.memset(MT[:, CI:C], 0.0).then_inc(pad_ready, 1)
            nc.gpsimd.memset(identity[:, :], 0.0).then_inc(identity_ready, 1)
            pool.wait_ge(identity_ready, 1)
            nc.gpsimd.affine_select(out=identity[:, :], in_=identity[:, :], compare_op=ALU.not_equal, fill=1.0,
                                    base=0, pattern=[[-1, C]], channel_multiplier=1).then_inc(identity_ready, 1)

            def residual(b, g):
                nc.gpsimd.tensor_tensor(Zres[:, columns(g)], Z[:, columns(g)],
                                        w[:, B_C:B_C + 1].broadcast_to([C, BANK]), ALU.add).then_inc(zres_ready, 1)

            def low_x(b):
                pool.wait_ge(x_hi, b)
                nc.gpsimd.tensor_tensor(X_lo[:, :], X[:, :], X_hi[:, :].bitcast(F32),
                                        ALU.subtract).then_inc(x_lo, 1)

            def low_z(b):
                pool.wait_ge(z_hi, b)
                nc.gpsimd.tensor_tensor(Z_lo[:, :], Z[:, :], Z_hi[:, :].bitcast(F32),
                                        ALU.subtract).then_inc(z_lo, 1)

            pool.wait_ge(w_loaded, 16)
            nc.gpsimd.tensor_scalar(phi_w[:, :], w[:, W_P:W_P + C], float(C) ** -0.5, None,
                                    ALU.mult).then_inc(phi_w_ready, 1)
            nc.gpsimd.tensor_scalar(phi_b[:, :], w[:, B_P:B_P + 1], float(C) ** -0.5, None,
                                    ALU.mult).then_inc(phi_w_ready, 1)
            pool.wait_ge(w_hi, 2)
            pool.wait_ge(phi_w_ready, 2)
            nc.gpsimd.tensor_tensor(T_w_lo[:, :], w[:, W_T:W_T + C], T_w_hi[:, :].bitcast(F32),
                                    ALU.subtract).then_inc(w_lo, 1)
            nc.gpsimd.tensor_tensor(phi_w_lo[:, :], phi_w[:, :], phi_w_hi[:, :].bitcast(F32),
                                    ALU.subtract).then_inc(w_lo, 1)
            pool.wait_ge(z_ready, 1)
            for g in range(GROUPS):
                residual(0, g)
            low_x(1)
            low_z(1)

            def finish(b, g):
                pool.wait_ge(numer_copied, b * GROUPS + g + 1)
                nc.gpsimd.tensor_tensor(result[:, g, :], attended[:, g, :], Zres[:, columns(g)],
                                        ALU.add).then_inc(result_ready, 1)

            def image(b, has_next):
                for g in range(GROUPS):
                    finish(b - 1, g)
                    pool.wait_ge(stored[g], b * 16)
                    residual(b, g)
                    if g == 0 and has_next:
                        low_x(b + 1)
                if has_next:
                    low_z(b + 1)

            with pool.Fori(1, IMAGES - 1) as b:
                image(b, True)
            image(IMAGES - 1, False)


def kernel(x, L0_conv_g_w, L0_conv_g_b, L0_conv_theta_w, L0_conv_theta_b, L0_conv_phi_w, L0_conv_phi_b,
           L0_conv_out_w, L0_conv_out_b, L1_conv_theta_w, L1_conv_theta_b, L1_conv_phi_w, L1_conv_phi_b,
           L1_conv_conv1_w, L1_conv_conv1_b):
    import numpy as np
    import concourse.bacc as bacc
    from concourse.bass_utils import run_bass_kernel_spmd

    n, c, h, wd = x.shape
    arrays = {
        "x_dram": np.ascontiguousarray(x.reshape(n, c, h * wd)),
        "pg_weights_dram": np.concatenate([L0_conv_phi_w.T, L0_conv_g_w.T], axis=1),
        "pg_bias_dram": np.concatenate([L0_conv_phi_b, L0_conv_g_b])[None, :],
        "inner_dram": np.concatenate([L0_conv_theta_w, L0_conv_out_w.T, L0_conv_theta_b[:, None]], axis=1),
        "weights_dram": np.concatenate(
            [L1_conv_theta_w.T, L1_conv_phi_w.T, L1_conv_conv1_w.T,
             L1_conv_theta_b[:, None], L1_conv_phi_b[:, None], L1_conv_conv1_b[:, None],
             L0_conv_out_b[:, None]], axis=1),
    }
    nc = bacc.Bacc("TRN2", target_bir_lowering=False, num_devices=1)
    args = [nc.dram_tensor(name, a.shape, mybir.dt.from_np(a.dtype), kind="ExternalInput").ap()
            for name, a in arrays.items()]
    args.append(nc.dram_tensor("out_dram", (n, c, h * wd), F32, kind="ExternalOutput").ap())
    build(nc, *args)
    r = run_bass_kernel_spmd(nc, [arrays], core_ids=[0])
    return r.results[0]["out_dram"].reshape(n, c, h, wd)
```

```python
from contextlib import ExitStack

import concourse.bass as bass
from concourse import mybir

F32 = mybir.dt.float32
F32R = mybir.dt.float32r
BF16 = mybir.dt.bfloat16
ALU = mybir.AluOpType
ACT = mybir.ActivationFunctionType
AX = mybir.AxisListType

IMAGES = 4
C = 128
CI = 64
PIX = 1024
TILE = 128
TILES = PIX // TILE
BANK = 512
GROUPS = PIX // BANK
GT = TILES // GROUPS
PIECES = 4
CHUNKS_PER_PIECE = TILES // PIECES
HALVES = PIX // BANK
CHUNKS_PER_HALF = TILES // HALVES
PIECES_PER_HALF = PIECES // HALVES

P_BUFFERS = 4
LAST_COLS = BANK - TILE
LAST_EARLY = 2
WARM_UP = 28

W_T, W_P, W_C = 0, C, 2 * C
B_T, B_P, B_C, B_O = 3 * C, 3 * C + 1, 3 * C + 2, 3 * C + 3
W_COLS = 3 * C + 4
I_T, I_O, I_TB = 0, C, 2 * C
I_COLS = 2 * C + 1


def build(nc, x, pg_weights, pg_bias, inner, weights, out):
    with ExitStack() as ctx:
        def sb(name, shape, dt=F32):
            return ctx.enter_context(nc.sbuf_tensor(name, shape, dt))

        def sem(name):
            return ctx.enter_context(nc.semaphore(name))

        pg_w = sb("pg_w", [C, C])
        w = sb("w", [C, W_COLS])
        wi = sb("wi", [CI, I_COLS])
        pg_b = sb("pg_b", [C, C])
        phi_w = sb("phi_w", [C, C])
        phi_b = sb("phi_b", [C, 1])
        T_w_hi, T_w_lo = sb("T_w_hi", [C, C], F32R), sb("T_w_lo", [C, C], F32R)
        phi_w_hi, phi_w_lo = sb("phi_w_hi", [C, C], F32R), sb("phi_w_lo", [C, C], F32R)
        identity = sb("identity", [C, C])
        table = sb("table", [C, 1])
        idle = sb("idle", [C, C], BF16)
        X_first = sb("X_first", [C, PIX])
        X = sb("X", [C, PIX])
        X_hi, X_lo = sb("X_hi", [C, PIX], F32R), sb("X_lo", [C, PIX], F32R)
        pgT = sb("pgT", [C, TILES, C])
        MT = sb("MT", [CI, C])
        R = sb("R", [CI, C])
        AT = sb("AT", [C, C])
        AT_hi, AT_lo = sb("AT_hi", [C, C], F32R), sb("AT_lo", [C, C], F32R)
        d = sb("d", [C, 1])
        Z = sb("Z", [C, PIX])
        Z_hi, Z_lo = sb("Z_hi", [C, PIX], F32R), sb("Z_lo", [C, PIX], F32R)
        Zres = sb("Zres", [C, PIX])
        T_hi, T_lo = sb("T_hi", [C, PIX], F32R), sb("T_lo", [C, PIX], F32R)
        Phi_hi, Phi_lo = sb("Phi_hi", [C, PIX], F32R), sb("Phi_lo", [C, PIX], F32R)
        V_hi, V_lo = sb("V_hi", [C, TILES * C], F32R), sb("V_lo", [C, TILES * C], F32R)
        negmax = sb("negmax", [C, TILES])
        den = sb("den", [C, TILES])
        rden = sb("rden", [C, TILES])
        P = sb("P", [C, P_BUFFERS, PIX])
        PT_hi = sb("PT_hi", [C, GROUPS, TILES, BANK], F32R)
        PT_lo = sb("PT_lo", [C, GROUPS, TILES, BANK], F32R)
        V_last = sb("V_last", [C, TILES * C])
        PT_last = sb("PT_last", [C, TILES, TILE])
        attended = sb("attended", [C, GROUPS, BANK])
        result = sb("result", [C, GROUPS, BANK])

        ring = ctx.enter_context(nc.psum_tensor("ring", [C, 3, PIX], F32))
        numer, small = ring[:, 2, 0:BANK], ring[:, 2, BANK:PIX]
        turned = ctx.enter_context(nc.psum_tensor("turned", [C, PIX], F32))

        last_rows = small[:, 0:LAST_COLS]
        last_tile = ring[:, 1, 0:TILE]

        S_SLOT = [1, 0, 1, 1, 0, 0, 0, 1]
        PG_SLOT, M_SLOT, V_SLOT, AX_SLOT, T_SLOT, PHI_SLOT = 0, 0, 1, 1, 0, 1
        FIRST_S_SLOT = [1, 0, 2, 1, 0, 0, 0, 1]
        LAST_S_SLOT = [0, 1, 0, 1, 0, 0, 1, 0]
        LAST_V_SLOT = 1

        pg_w_loaded, pg_b_loaded, wi_loaded, w_loaded = (
            sem(n + "_loaded") for n in ("pg_w", "pg_b", "wi", "w"))
        first_loaded = [sem(f"first_loaded{h}") for h in range(HALVES)]
        x_loaded = sem("x_loaded")
        idle_ready = sem("idle_ready")
        identity_ready, pad_ready, table_ready = sem("identity_ready"), sem("pad_ready"), sem("table_ready")
        phi_w_ready, w_hi, w_lo = sem("phi_w_ready"), sem("w_hi"), sem("w_lo")
        pg_ready, pg_copied = sem("pg_ready"), sem("pg_copied")
        m_ready, m_copied = sem("m_ready"), sem("m_copied")
        r_ready, r_copied = sem("r_ready"), sem("r_copied")
        a_ready, a_copied = sem("a_ready"), sem("a_copied")
        x_hi, x_lo, a_lo, z_hi, z_lo = (sem(n) for n in ("x_hi", "x_lo", "a_lo", "z_hi", "z_lo"))
        ax_ready, t_ready, t_hi, phi_ready, phi_hi = (
            sem(n) for n in ("ax_ready", "t_ready", "t_hi", "phi_ready", "phi_hi"))
        z_ready, zres_ready, t_lo, phi_lo = sem("z_ready"), sem("zres_ready"), sem("t_lo"), sem("phi_lo")
        half = {n: sem("half_" + n) for n in ("pg", "pg_copied", "next_pg", "next_copied", "ax", "z",
                                              "t", "t_hi", "t_lo", "phi", "phi_hi", "phi_lo")}
        v_ready, v_hi, v_lo = sem("v_ready"), sem("v_hi"), sem("v_lo")
        scores_ready, max_ready, probs_ready = sem("scores_ready"), sem("max_ready"), sem("probs_ready")
        rden_ready, probs_normed = sem("rden_ready"), sem("probs_normed")
        turned_ready, turned_hi, turned_lo = sem("turned_ready"), sem("turned_hi"), sem("turned_lo")
        pieces_done, numer_copied, result_ready = sem("pieces_done"), sem("numer_copied"), sem("result_ready")
        stored = [sem(f"stored{g}") for g in range(GROUPS)]
        last_stored = sem("last_stored")
        v_joined, last_turned = sem("v_joined"), [sem(f"last_turned{h}") for h in range(HALVES)]

        block = ctx.enter_context(nc.Block())

        def columns(h):
            return slice(h * BANK, (h + 1) * BANK)

        def half_chunks(h):
            return slice(h * CHUNKS_PER_HALF, (h + 1) * CHUNKS_PER_HALF)

        def half_range(h):
            return range(h * CHUNKS_PER_HALF, (h + 1) * CHUNKS_PER_HALF)

        def over_images(eng, image):
            image(0, False, True)
            with eng.Fori(1, IMAGES - 1) as b:
                image(b, True, True)
            image(IMAGES - 1, True, False)

        @block.sync
        def _(sp):
            for h in range(HALVES):
                sp.dma_start(X_first[:, columns(h)], x[0, :, columns(h)]).then_inc(first_loaded[h], 16)
            sp.dma_start(wi[:, :], inner).then_inc(wi_loaded, 16)
            sp.dma_start(X[:, :], x[1]).then_inc(x_loaded, 16)

            def load(b):
                sp.wait_ge(z_ready, b)
                sp.dma_start(X[:, :], x[b]).then_inc(x_loaded, 16)

            def store(b):
                for g in range(GROUPS):
                    sp.wait_ge(result_ready, b * GROUPS + g + 1)
                    sp.dma_start(out[b, :, columns(g)], result[:, g, :]).then_inc(stored[g], 16)

            with sp.Fori(0, IMAGES - 2) as b:
                load(b + 2)
                store(b)
            store(IMAGES - 2)
            parts = ((0, slice(0, BANK)), (1, slice(0, LAST_COLS)), (1, slice(LAST_COLS, BANK)))
            for n, (g, cols) in enumerate(parts):
                sp.wait_ge(result_ready, (IMAGES - 1) * GROUPS + n + 1)
                sp.dma_start(out[IMAGES - 1, :, g * BANK + cols.start:g * BANK + cols.stop],
                             result[:, g, cols]).then_inc(last_stored, 16)
            for g in range(GROUPS):
                sp.wait_ge(stored[g], 16 * (IMAGES - 1))
            sp.wait_ge(last_stored, 16 * len(parts))

        @block.tensor
        def _(pe):
            def phi_g_chunks(to, source, chunks):
                for j in chunks:
                    mm = nc.tensor.matmul(to[:, j * C:(j + 1) * C], source[:, j * TILE:(j + 1) * TILE],
                                          pg_w[:, :], start=True, stop=True)
                return mm

            def phi_g(b):
                pe.wait_ge(x_loaded, b * 16)
                phi_g_chunks(ring[:, PG_SLOT, :], X, range(TILES)).then_inc(pg_ready, 1)

            def inner_chunks(chunks):
                for j in chunks:
                    mm = nc.tensor.matmul(ring[0:CI, M_SLOT, 0:CI], pgT[:, j, CI:C], pgT[:, j, 0:CI],
                                          start=(j == 0), stop=(j == TILES - 1))
                return mm

            def inner_product(b):
                pe.wait_ge(pg_copied, b + 1)
                inner_chunks(range(TILES)).then_inc(m_ready, 1)

            def out_times_inner(b):
                pe.wait_ge(m_copied, b + 1)
                nc.tensor.matmul(small[:, 0:C], MT[:, :], wi[:, I_O:I_O + C],
                                 start=True, stop=True).then_inc(r_ready, 1)

            def fold(b):
                pe.wait_ge(r_copied, b + 1)
                nc.tensor.matmul(small[:, 0:C], wi[:, I_T:I_T + C], R[:, :], start=True, stop=False)
                nc.tensor.matmul(small[:, 0:C], identity[:, :], identity[:, :], start=False, stop=True)
                nc.tensor.matmul(small[:, C:C + 1], R[:, :], wi[:, I_TB:I_TB + 1],
                                 start=True, stop=True).then_inc(a_ready, 1)

            def conv_half(slot, weight, source, h, done):
                nc.tensor.matmul(ring[:, slot, columns(h)], weight, source[:, columns(h)],
                                 start=True, stop=True).then_inc(done, 1)

            def three_passes(slot, lefts, rights, done, right_lo_made=None):
                (left_hi, left_lo), (right_hi, right_lo) = lefts, rights
                for n, (left, right) in enumerate(((left_hi, right_hi), (left_lo, right_hi), (left_hi, right_lo))):
                    if n == 2 and right_lo_made is not None:
                        pe.wait_ge(*right_lo_made)
                    for h in range(HALVES):
                        mm = nc.tensor.matmul(ring[:, slot, columns(h)], left, right[:, columns(h)],
                                              start=(n == 0), stop=(n == 2))
                mm.then_inc(done, 1)

            def values(b, slot):
                pe.wait_ge(probs_ready, b * TILES + 4)
                for j in range(TILES):
                    mm = nc.tensor.matmul(ring[:, slot, j * C:(j + 1) * C], Z[:, j * TILE:(j + 1) * TILE],
                                          w[:, W_C:W_C + C], start=True, stop=True)
                mm.then_inc(v_ready, 1)

            def fold_x(b):
                pe.wait_ge(x_lo, b)
                pe.wait_ge(a_lo, b)
                pe.wait_ge(v_lo, b)
                three_passes(AX_SLOT, (AT_hi[:, :], AT_lo[:, :]), (X_hi, X_lo), ax_ready)

            def theta(b):
                pe.wait_ge(w_lo, 2)
                pe.wait_ge(probs_ready, (b - 1) * TILES + 7)
                pe.wait_ge(z_hi, b)
                three_passes(T_SLOT, (T_w_hi[:, :], T_w_lo[:, :]), (Z_hi, Z_lo), t_ready, (z_lo, b))

            def phi(b):
                pe.wait_ge(probs_ready, b * TILES)
                three_passes(PHI_SLOT, (phi_w_hi[:, :], phi_w_lo[:, :]), (Z_hi, Z_lo), phi_ready)

            def first_scores_half(h):
                for n, (left, right) in enumerate(((T_hi, Phi_hi), (T_lo, Phi_hi), (T_hi, Phi_lo))):
                    mm = nc.tensor.matmul(ring[:, S_SLOT[0], columns(h)], left[:, 0:TILE], right[:, columns(h)],
                                          start=(n == 0), stop=(n == 2))
                return mm

            def scores(t, slots=S_SLOT, phi_lo_made=None):
                rows = slice(t * TILE, (t + 1) * TILE)
                three_passes(slots[t], (T_hi[:, rows], T_lo[:, rows]), (Phi_hi, Phi_lo), scores_ready,
                             phi_lo_made)

            def turn(b, t, h, first=False):
                if h == 0:
                    pe.wait_ge(probs_normed, b * TILES + t + 1)
                if not first:
                    pe.wait_ge(turned_lo, (b * TILES + t - 1) * HALVES + h + 1)
                for j in half_range(h):
                    mm = nc.tensor.transpose(turned[:, j * TILE:(j + 1) * TILE],
                                             P[:, t % P_BUFFERS, j * TILE:(j + 1) * TILE], identity[:, :])
                mm.then_inc(turned_ready, 1)

            def turn_tile(b, t, first=False):
                for h in range(HALVES):
                    turn(b, t, h, first)

            def attend_last(j):
                rows = slice(0, LAST_COLS)
                chunk = slice(j * C, (j + 1) * C)
                for n, (left, right) in enumerate(((V_hi, PT_hi), (V_hi, PT_lo), (V_lo, PT_hi))):
                    mm = nc.tensor.matmul(last_rows, left[:, chunk], right[:, GROUPS - 1, j, rows],
                                          start=(j == 0 and n == 0), stop=(j == TILES - 1 and n == 2))
                return mm

            def attend(b, g, i, first=False):
                if i % PIECES_PER_HALF == 0:
                    h = i // PIECES_PER_HALF
                    pe.wait_ge(turned_lo, (b * TILES + (g + 1) * GT - 1) * HALVES + h + 1)
                if i == 0:
                    if g == 0:
                        pe.wait_ge(v_lo, b + 1)
                    if not first:
                        pe.wait_ge(numer_copied, b * GROUPS + g)
                for j in range(i * CHUNKS_PER_PIECE, (i + 1) * CHUNKS_PER_PIECE):
                    chunk = slice(j * C, (j + 1) * C)
                    for n, (left, right) in enumerate(((V_hi, PT_hi), (V_hi, PT_lo), (V_lo, PT_hi))):
                        mm = nc.tensor.matmul(numer[:, :], left[:, chunk], right[:, g, j, :],
                                              start=(j == 0 and n == 0), stop=(j == TILES - 1 and n == 2))
                mm.then_inc(pieces_done, 1)

            pe.wait_ge(idle_ready, 1)
            for _ in range(WARM_UP):
                nc.tensor.matmul(small[:, 0:C], idle[:, :], idle[:, :], start=True, stop=True)
            pe.wait_ge(pg_w_loaded, 16)
            for h in range(HALVES):
                pe.wait_ge(first_loaded[h], 16)
                phi_g_chunks(ring[:, PG_SLOT, :], X_first,
                             half_range(h)).then_inc(half["pg"] if h == 0 else pg_ready, 1)
            pe.wait_ge(half["pg_copied"], 1)
            inner_chunks(half_range(0))
            pe.wait_ge(x_loaded, 16)
            phi_g_chunks(turned, X, range(0, 2))
            pe.wait_ge(pg_copied, 1)
            inner_chunks(half_range(1)).then_inc(m_ready, 1)
            phi_g_chunks(turned, X, range(2, 4)).then_inc(half["next_pg"], 1)
            pe.wait_ge(pad_ready, 1)
            pe.wait_ge(identity_ready, 2)
            pe.wait_ge(wi_loaded, 16)
            out_times_inner(0)
            phi_g_chunks(turned, X, range(4, 6))
            fold(0)
            phi_g_chunks(turned, X, range(6, TILES)).then_inc(pg_ready, 1)
            pe.wait_ge(a_copied, 1)
            for h in range(HALVES):
                conv_half(AX_SLOT, AT[:, :], X_first, h, half["ax"])
            pe.wait_ge(phi_w_ready, 2)
            pe.wait_ge(half["z"], 1)
            conv_half(T_SLOT, w[:, W_T:W_T + C], Z, 0, half["t"])
            pe.wait_ge(z_ready, 1)
            conv_half(PHI_SLOT, phi_w[:, :], Z, 0, half["phi"])
            conv_half(PHI_SLOT, phi_w[:, :], Z, 1, half["phi"])
            conv_half(T_SLOT, w[:, W_T:W_T + C], Z, 1, half["t"])

            def image(b, has_prev, has_next):
                if not has_next:
                    return last_image(b)
                if has_prev:
                    pe.wait_ge(t_lo, b + 1)
                    phi_g(b + 1)
                    turn_tile(b - 1, 7)
                    pe.wait_ge(phi_lo, b + 1)
                    scores(0)
                    attend(b - 1, 1, 0)
                    pe.wait_ge(pg_copied, b + 2)
                    scores(1)
                    attend(b - 1, 1, 1)
                else:
                    for h in range(HALVES):
                        pe.wait_ge(half["phi_lo"] if h == 0 else phi_lo, 1)
                        pe.wait_ge(half["t_lo"], 1)
                        mm = first_scores_half(h)
                    mm.then_inc(scores_ready, 1)
                    pe.wait_ge(t_lo, 1)
                    scores(1)
                    scores(2, FIRST_S_SLOT)
                pe.wait_ge(probs_ready, b * TILES + 1)
                if has_prev:
                    scores(2)
                else:
                    scores(3)
                    pe.wait_ge(pg_copied, 2)
                turn(b, 0, 0, first=not has_prev)
                if has_prev:
                    attend(b - 1, 1, 2)
                turn(b, 0, 1, first=not has_prev)
                pe.wait_ge(probs_ready, b * TILES + 2)
                inner_product(b + 1)
                pe.wait_ge(probs_ready, b * TILES + 3)
                if has_prev:
                    scores(3)
                turn(b, 1, 0)
                if has_prev:
                    attend(b - 1, 1, 3)
                turn(b, 1, 1)
                pe.wait_ge(a_copied, b + 1)
                out_times_inner(b + 1)
                scores(4)
                turn_tile(b, 2)
                values(b, V_SLOT)
                fold(b + 1)
                pe.wait_ge(probs_ready, b * TILES + 5)
                scores(5)
                turn_tile(b, 3)
                fold_x(b + 1)
                attend(b, 0, 0, first=not has_prev)
                pe.wait_ge(probs_ready, b * TILES + 6)
                scores(6)
                turn(b, 4, 0)
                attend(b, 0, 1)
                turn(b, 4, 1)
                pe.wait_ge(z_ready, b + 2)
                scores(7)
                turn(b, 5, 0)
                attend(b, 0, 2)
                turn(b, 5, 1)
                theta(b + 1)
                turn_tile(b, 6)
                phi(b + 1)
                attend(b, 0, 3)

            def last_image(b):
                turn_tile(b - 1, 7)
                pe.wait_ge(t_lo, b + 1)
                pe.wait_ge(phi_hi, b)
                scores(0, LAST_S_SLOT, (phi_lo, b + 1))
                attend(b - 1, 1, 0)
                scores(1, LAST_S_SLOT)
                attend(b - 1, 1, 1)
                pe.wait_ge(probs_ready, b * TILES + 1)
                scores(2, LAST_S_SLOT)
                turn(b, 0, 0)
                attend(b - 1, 1, 2)
                turn(b, 0, 1)
                pe.wait_ge(probs_ready, b * TILES + 2)
                scores(3, LAST_S_SLOT)
                turn(b, 1, 0)
                attend(b - 1, 1, 3)
                turn(b, 1, 1)
                pe.wait_ge(probs_ready, b * TILES + 3)
                scores(4, LAST_S_SLOT)
                turn_tile(b, 2)
                values(b, LAST_V_SLOT)
                pe.wait_ge(probs_ready, b * TILES + 5)
                scores(5, LAST_S_SLOT)
                turn_tile(b, 3)
                pe.wait_ge(v_lo, b + 1)
                scores(6, LAST_S_SLOT)
                attend(b, 0, 0)
                turn_tile(b, 4)
                pe.wait_ge(probs_ready, b * TILES + 6)
                scores(7, LAST_S_SLOT)
                turn(b, 5, 0)
                attend(b, 0, 1)
                turn(b, 5, 1)
                attend(b, 0, 2)
                turn_tile(b, 6)
                attend(b, 0, 3)

            over_images(pe, image)
            pe.wait_ge(turned_lo, (IMAGES * TILES - 1) * HALVES)
            for j in range(LAST_EARLY):
                attend_last(j)
            for h in range(HALVES):
                turn(IMAGES - 1, 7, h)
            for j in range(LAST_EARLY, TILES):
                mm = attend_last(j)
            mm.then_inc(pieces_done, 1)
            pe.wait_ge(v_joined, 1)
            for h in range(HALVES):
                pe.wait_ge(last_turned[h], 1)
                for j in half_range(h):
                    mm = nc.tensor.matmul(last_tile, V_last[:, j * C:(j + 1) * C], PT_last[:, j, :],
                                          start=(j == 0), stop=(j == TILES - 1))
            mm.then_inc(pieces_done, 1)

        @block.scalar
        def _(act):
            act.dma_start(pg_w[:, :], pg_weights).then_inc(pg_w_loaded, 16)
            act.dma_start(pg_b[:, :], pg_bias.broadcast_to([C, C])).then_inc(pg_b_loaded, 16)
            act.dma_start(w[:, :], weights).then_inc(w_loaded, 16)
            act.wait_ge(table_ready, 1)
            nc.scalar.activation(table[:, :], table[:, :], ACT.Exp)

            def copy_m(b):
                act.wait_ge(m_ready, b + 1)
                nc.scalar.activation(MT[:, 0:CI], ring[0:CI, M_SLOT, 0:CI], ACT.Copy,
                                     scale=1.0 / PIX).then_inc(m_copied, 1)

            def copy_r(b):
                act.wait_ge(r_ready, b + 1)
                nc.scalar.activation(R[:, :], small[0:CI, 0:C], ACT.Copy).then_inc(r_copied, 1)

            def copy_a(b, to):
                act.wait_ge(a_ready, b + 1)
                nc.scalar.activation(d[:, :], small[:, C:C + 1], ACT.Identity, bias=w[:, B_O:B_O + 1])
                nc.scalar.activation(to[:, :], small[:, 0:C], ACT.Copy).then_inc(a_copied, 1)

            def high_x(b, first):
                act.wait_ge(x_loaded, b * 16)
                if not first:
                    act.wait_ge(ax_ready, b - 1)
                nc.scalar.activation(X_hi[:, :], X[:, :], ACT.Copy).then_inc(x_hi, 1)

            def make_z(b, first):
                act.wait_ge(zres_ready, b * GROUPS)
                act.wait_ge(v_ready, b)
                if not first:
                    act.wait_ge(z_lo, b - 1)
                act.wait_ge(ax_ready, b)
                nc.scalar.activation(Z[:, :], ring[:, AX_SLOT, :], ACT.Identity, bias=d[:, :]).then_inc(z_ready, 1)

            def high_z(b, first):
                act.wait_ge(z_ready, b + 1)
                if not first:
                    act.wait_ge(phi_ready, b - 1)
                nc.scalar.activation(Z_hi[:, :], Z[:, :], ACT.Copy).then_inc(z_hi, 1)

            def high(hi, slot, bias, cols, done):
                nc.scalar.activation(hi[:, cols], ring[:, slot, cols], ACT.Identity, bias=bias).then_inc(done, 1)

            def high_t(b):
                act.wait_ge(t_ready, b)
                act.wait_ge(scores_ready, b * TILES)
                high(T_hi, T_SLOT, w[:, B_T:B_T + 1], slice(0, PIX), t_hi)

            def high_phi(b):
                act.wait_ge(phi_ready, b)
                high(Phi_hi, PHI_SLOT, phi_b[:, :], slice(0, PIX), phi_hi)

            def high_v(b, has_prev, slot):
                if has_prev:
                    act.wait_ge(pieces_done, b * PIECES * GROUPS)
                act.wait_ge(v_ready, b + 1)
                nc.scalar.activation(V_hi[:, :], ring[:, slot, :], ACT.Copy).then_inc(v_hi, 1)

            def exps(b, t, has_prev, slots):
                if t >= P_BUFFERS or has_prev:
                    act.wait_ge(turned_ready, (b * TILES + t - P_BUFFERS + 1) * HALVES)
                act.wait_ge(max_ready, b * TILES + t + 1)
                nc.scalar.activation(P[:, t % P_BUFFERS, :], ring[:, slots[t], :], ACT.Exp, bias=negmax[:, t:t + 1],
                                     accum_out=den[:, t:t + 1]).then_inc(probs_ready, 1)

            def high_turned(b, t, h, has_prev=False):
                g, k = divmod(t, GT)
                if has_prev and k == 0 and h == 0:
                    act.wait_ge(pieces_done, (b - 1) * PIECES * GROUPS + (g + 1) * PIECES)
                act.wait_ge(turned_ready, (b * TILES + t) * HALVES + h + 1)
                nc.scalar.activation(PT_hi[:, g, half_chunks(h), k * TILE:(k + 1) * TILE],
                                     turned[:, columns(h)].rearrange("p (j r) -> p j r", j=CHUNKS_PER_HALF),
                                     ACT.Copy).then_inc(turned_hi, 1)

            def copy_numer(b, g):
                act.wait_ge(pieces_done, (b * GROUPS + g + 1) * PIECES)
                act.wait_ge(zres_ready, b * GROUPS + g + 1)
                nc.scalar.activation(attended[:, g, :], numer[:, :], ACT.Copy).then_inc(numer_copied, 1)

            def high_t_half(h):
                act.wait_ge(half["t"], h + 1)
                high(T_hi, T_SLOT, w[:, B_T:B_T + 1], columns(h), half["t_hi"])

            def high_phi_half(h):
                act.wait_ge(half["phi"], h + 1)
                high(Phi_hi, PHI_SLOT, phi_b[:, :], columns(h), half["phi_hi"])

            act.wait_ge(w_loaded, 16)
            nc.scalar.activation(T_w_hi[:, :], w[:, W_T:W_T + C], ACT.Copy).then_inc(w_hi, 1)
            copy_m(0)
            copy_r(0)
            copy_a(0, AT)
            high_x(1, first=True)
            act.wait_ge(phi_w_ready, 2)
            nc.scalar.activation(phi_w_hi[:, :], phi_w[:, :], ACT.Copy).then_inc(w_hi, 1)
            high_t_half(0)
            high_phi_half(0)
            high_phi_half(1)
            high_t_half(1)

            def image(b, has_prev, has_next):
                slots = LAST_S_SLOT if not has_next else S_SLOT if has_prev else FIRST_S_SLOT
                if has_prev:
                    high_turned(b - 1, 7, 0)
                    high_turned(b - 1, 7, 1)
                exps(b, 0, has_prev, slots)
                exps(b, 1, has_prev, slots)
                for t in range(2, TILES):
                    high_turned(b, t - 2, 0, has_prev)
                    if t == 4:
                        high_turned(b, t - 2, 1)
                    exps(b, t, has_prev, slots)
                    if t == 4:
                        high_v(b, has_prev, V_SLOT if has_next else LAST_V_SLOT)
                    else:
                        high_turned(b, t - 2, 1)
                    if has_prev and t == 3:
                        copy_numer(b - 1, 1)
                    if not has_next:
                        continue
                    if t == 2:
                        copy_m(b + 1)
                    if t == 3:
                        copy_r(b + 1)
                        if has_prev:
                            high_x(b + 1, first=False)
                    if t == 4:
                        act.wait_ge(z_ready, b + 1)
                        copy_a(b + 1, AT_hi)
                    if t == 5:
                        make_z(b + 1, first=not has_prev)
                        high_z(b + 1, first=not has_prev)
                if has_next:
                    high_t(b + 1)
                high_turned(b, 6, 0)
                high_turned(b, 6, 1)
                if has_next:
                    high_phi(b + 1)
                    copy_numer(b, 0)

            over_images(act, image)
            act.wait_ge(turned_ready, (IMAGES * TILES - 1) * HALVES + 1)
            nc.scalar.activation(PT_last[:, half_chunks(0), :], turned[:, columns(0)].rearrange(
                "p (j r) -> p j r", j=CHUNKS_PER_HALF), ACT.Copy).then_inc(last_turned[0], 1)

        @block.vector
        def _(dve):
            nc.vector.memset(idle[:, :], 0.0).then_inc(idle_ready, 1)
            nc.vector.memset(table[:, :], 0.0).then_inc(table_ready, 1)

            def copy_pg_chunks(source, chunks, count, done):
                nc.vector.tensor_tensor(pgT[:, chunks, :], source.rearrange("p (j c) -> p j c", j=count),
                                        pg_b[:, :].rearrange("p (a c) -> p a c", a=1).broadcast_to([C, count, C]),
                                        ALU.add).then_inc(done, 1)

            def copy_pg(b):
                dve.wait_ge(pg_ready, b + 1)
                copy_pg_chunks(ring[:, PG_SLOT, :], slice(0, TILES), TILES, pg_copied)

            def low_a(b):
                dve.wait_ge(a_copied, b + 1)
                nc.vector.tensor_tensor(AT_lo[:, :], small[:, 0:C], AT_hi[:, :].bitcast(F32),
                                        ALU.subtract).then_inc(a_lo, 1)

            def low(lo, hi, slot, bias, cols, done):
                nc.vector.scalar_tensor_tensor(out=lo[:, cols], in0=ring[:, slot, cols], scalar=bias,
                                               in1=hi[:, cols].bitcast(F32), op0=ALU.add,
                                               op1=ALU.subtract).then_inc(done, 1)

            def low_t(b):
                dve.wait_ge(t_hi, b)
                low(T_lo, T_hi, T_SLOT, w[:, B_T:B_T + 1], slice(0, PIX), t_lo)

            def low_phi(b):
                dve.wait_ge(phi_hi, b)
                low(Phi_lo, Phi_hi, PHI_SLOT, phi_b[:, :], slice(0, PIX), phi_lo)

            def low_v(b, slot):
                dve.wait_ge(v_hi, b + 1)
                nc.vector.tensor_tensor(V_lo[:, :], ring[:, slot, :], V_hi[:, :].bitcast(F32),
                                        ALU.subtract).then_inc(v_lo, 1)

            def row_max(b, t, slots):
                dve.wait_ge(scores_ready, b * TILES + t + 1)
                nc.vector.tensor_reduce(negmax[:, t:t + 1], ring[:, slots[t], :], AX.X, ALU.max,
                                        negate=True).then_inc(max_ready, 1)

            def norm(b, t):
                dve.wait_ge(probs_ready, b * TILES + t + 1)
                nc.vector.reciprocal(rden[:, t:t + 1], den[:, t:t + 1]).then_inc(rden_ready, 1)
                dve.wait_ge(rden_ready, b * TILES + t + 1)
                nc.vector.tensor_scalar(P[:, t % P_BUFFERS, :], P[:, t % P_BUFFERS, :], rden[:, t:t + 1], None,
                                        ALU.mult).then_inc(probs_normed, 1)

            def low_turned(b, t, h):
                g, k = divmod(t, GT)
                rows = slice(k * TILE, (k + 1) * TILE)
                dve.wait_ge(turned_hi, (b * TILES + t) * HALVES + h + 1)
                nc.vector.tensor_tensor(PT_lo[:, g, half_chunks(h), rows],
                                        turned[:, columns(h)].rearrange("p (j r) -> p j r", j=CHUNKS_PER_HALF),
                                        PT_hi[:, g, half_chunks(h), rows].bitcast(F32),
                                        ALU.subtract).then_inc(turned_lo, 1)

            def finish_last_group(source, g, cols, count):
                dve.wait_ge(pieces_done, (IMAGES - 1) * GROUPS * PIECES + count)
                dve.wait_ge(zres_ready, IMAGES * GROUPS)
                pixels = slice(g * BANK + cols.start, g * BANK + cols.stop)
                nc.vector.tensor_tensor(result[:, g, cols], source, Zres[:, pixels],
                                        ALU.add).then_inc(result_ready, 1)

            def low_t_half(h):
                dve.wait_ge(half["t_hi"], h + 1)
                low(T_lo, T_hi, T_SLOT, w[:, B_T:B_T + 1], columns(h), t_lo if h else half["t_lo"])

            def low_phi_half(h):
                dve.wait_ge(half["phi_hi"], h + 1)
                low(Phi_lo, Phi_hi, PHI_SLOT, phi_b[:, :], columns(h), phi_lo if h else half["phi_lo"])

            dve.wait_ge(pg_b_loaded, 16)
            for h in range(HALVES):
                dve.wait_ge(half["pg"] if h == 0 else pg_ready, 1)
                copy_pg_chunks(ring[:, PG_SLOT, columns(h)], half_chunks(h), CHUNKS_PER_HALF,
                               half["pg_copied"] if h == 0 else pg_copied)
            dve.wait_ge(m_ready, 1)
            dve.wait_ge(half["next_pg"], 1)
            copy_pg_chunks(turned[:, columns(0)], half_chunks(0), CHUNKS_PER_HALF, half["next_copied"])
            dve.wait_ge(a_copied, 1)
            for h in range(HALVES):
                dve.wait_ge(half["ax"], h + 1)
                nc.vector.tensor_scalar(Z[:, columns(h)], ring[:, AX_SLOT, columns(h)], d[:, :], None,
                                        ALU.add).then_inc(z_ready if h else half["z"], 1)
            dve.wait_ge(pg_ready, 2)
            copy_pg_chunks(turned[:, columns(1)], half_chunks(1), CHUNKS_PER_HALF, pg_copied)
            low_t_half(0)
            low_phi_half(0)
            low_phi_half(1)
            low_t_half(1)

            def image(b, has_prev, has_next):
                slots = LAST_S_SLOT if not has_next else S_SLOT if has_prev else FIRST_S_SLOT
                if has_prev:
                    if has_next:
                        copy_pg(b + 1)
                    low_turned(b - 1, 7, 0)
                row_max(b, 0, slots)
                if has_prev:
                    low_turned(b - 1, 7, 1)
                for t in range(TILES - 1):
                    row_max(b, t + 1, slots)
                    if t >= 1:
                        low_turned(b, t - 1, 0)
                    norm(b, t)
                    if t >= 1:
                        low_turned(b, t - 1, 1)
                    if t == 3:
                        low_v(b, V_SLOT if has_next else LAST_V_SLOT)
                        if has_next:
                            low_a(b + 1)
                norm(b, 7)
                if has_next:
                    low_t(b + 1)
                low_turned(b, 6, 0)
                low_turned(b, 6, 1)
                if has_next:
                    low_phi(b + 1)

            over_images(dve, image)
            finish_last_group(numer[:, :], 0, slice(0, BANK), PIECES)
            dve.wait_ge(turned_ready, IMAGES * TILES * HALVES)
            nc.vector.tensor_copy(PT_last[:, half_chunks(1), :], turned[:, columns(1)].rearrange(
                "p (j r) -> p j r", j=CHUNKS_PER_HALF)).then_inc(last_turned[1], 1)
            finish_last_group(last_rows, 1, slice(0, LAST_COLS), PIECES + 1)
            finish_last_group(last_tile, 1, slice(LAST_COLS, BANK), PIECES + 2)

        @block.gpsimd
        def _(pool):
            nc.gpsimd.memset(MT[:, CI:C], 0.0).then_inc(pad_ready, 1)
            nc.gpsimd.memset(identity[:, :], 0.0).then_inc(identity_ready, 1)
            pool.wait_ge(identity_ready, 1)
            nc.gpsimd.affine_select(out=identity[:, :], in_=identity[:, :], compare_op=ALU.not_equal, fill=1.0,
                                    base=0, pattern=[[-1, C]], channel_multiplier=1).then_inc(identity_ready, 1)

            def residual(b, g):
                nc.gpsimd.tensor_tensor(Zres[:, columns(g)], Z[:, columns(g)],
                                        w[:, B_C:B_C + 1].broadcast_to([C, BANK]), ALU.add).then_inc(zres_ready, 1)

            def low_x(b):
                pool.wait_ge(x_hi, b)
                nc.gpsimd.tensor_tensor(X_lo[:, :], X[:, :], X_hi[:, :].bitcast(F32),
                                        ALU.subtract).then_inc(x_lo, 1)

            def low_z(b):
                pool.wait_ge(z_hi, b)
                nc.gpsimd.tensor_tensor(Z_lo[:, :], Z[:, :], Z_hi[:, :].bitcast(F32),
                                        ALU.subtract).then_inc(z_lo, 1)

            pool.wait_ge(w_loaded, 16)
            nc.gpsimd.tensor_scalar(phi_w[:, :], w[:, W_P:W_P + C], float(C) ** -0.5, None,
                                    ALU.mult).then_inc(phi_w_ready, 1)
            nc.gpsimd.tensor_scalar(phi_b[:, :], w[:, B_P:B_P + 1], float(C) ** -0.5, None,
                                    ALU.mult).then_inc(phi_w_ready, 1)
            pool.wait_ge(w_hi, 2)
            pool.wait_ge(phi_w_ready, 2)
            nc.gpsimd.tensor_tensor(T_w_lo[:, :], w[:, W_T:W_T + C], T_w_hi[:, :].bitcast(F32),
                                    ALU.subtract).then_inc(w_lo, 1)
            nc.gpsimd.tensor_tensor(phi_w_lo[:, :], phi_w[:, :], phi_w_hi[:, :].bitcast(F32),
                                    ALU.subtract).then_inc(w_lo, 1)
            pool.wait_ge(z_ready, 1)
            for g in range(GROUPS):
                residual(0, g)
            low_x(1)
            low_z(1)

            def finish(b, g):
                pool.wait_ge(numer_copied, b * GROUPS + g + 1)
                nc.gpsimd.tensor_tensor(result[:, g, :], attended[:, g, :], Zres[:, columns(g)],
                                        ALU.add).then_inc(result_ready, 1)

            def image(b, has_next):
                for g in range(GROUPS):
                    finish(b - 1, g)
                    pool.wait_ge(stored[g], b * 16)
                    residual(b, g)
                    if g == 0 and has_next:
                        low_x(b + 1)
                if has_next:
                    low_z(b + 1)

            with pool.Fori(1, IMAGES - 1) as b:
                image(b, True)
            image(IMAGES - 1, False)
            pool.wait_ge(v_lo, IMAGES)
            nc.gpsimd.tensor_tensor(V_last[:, :], V_hi[:, :].bitcast(F32), V_lo[:, :].bitcast(F32),
                                    ALU.add).then_inc(v_joined, 1)


def kernel(x, L0_conv_g_w, L0_conv_g_b, L0_conv_theta_w, L0_conv_theta_b, L0_conv_phi_w, L0_conv_phi_b,
           L0_conv_out_w, L0_conv_out_b, L1_conv_theta_w, L1_conv_theta_b, L1_conv_phi_w, L1_conv_phi_b,
           L1_conv_conv1_w, L1_conv_conv1_b):
    import numpy as np
    import concourse.bacc as bacc
    from concourse.bass_utils import run_bass_kernel_spmd

    n, c, h, wd = x.shape
    arrays = {
        "x_dram": np.ascontiguousarray(x.reshape(n, c, h * wd)),
        "pg_weights_dram": np.concatenate([L0_conv_phi_w.T, L0_conv_g_w.T], axis=1),
        "pg_bias_dram": np.concatenate([L0_conv_phi_b, L0_conv_g_b])[None, :],
        "inner_dram": np.concatenate([L0_conv_theta_w, L0_conv_out_w.T, L0_conv_theta_b[:, None]], axis=1),
        "weights_dram": np.concatenate(
            [L1_conv_theta_w.T, L1_conv_phi_w.T, L1_conv_conv1_w.T,
             L1_conv_theta_b[:, None], L1_conv_phi_b[:, None], L1_conv_conv1_b[:, None],
             L0_conv_out_b[:, None]], axis=1),
    }
    nc = bacc.Bacc("TRN2", target_bir_lowering=False, num_devices=1)
    args = [nc.dram_tensor(name, a.shape, mybir.dt.from_np(a.dtype), kind="ExternalInput").ap()
            for name, a in arrays.items()]
    args.append(nc.dram_tensor("out_dram", (n, c, h * wd), F32, kind="ExternalOutput").ap())
    build(nc, *args)
    r = run_bass_kernel_spmd(nc, [arrays], core_ids=[0])
    return r.results[0]["out_dram"].reshape(n, c, h, wd)
```
